# Optimizing a Trainium2 kernel written in Bass

```python
import numpy as np
import jax
import jax.numpy as jnp

def _softmax(x, axis=-1):
    return jax.nn.softmax(x, axis=axis)
def _gelu(x):
    return jax.nn.gelu(x, approximate=True)
def _silu(x):
    return jax.nn.silu(x)
def _sigmoid(x):
    return jax.nn.sigmoid(x)
def _layernorm(x, axis=-1, eps=1e-5):
    m = jnp.mean(x, axis=axis, keepdims=True)
    v = jnp.var(x, axis=axis, keepdims=True)
    return (x - m) / jnp.sqrt(v + eps)
def _scatter_add(tgt, idx, src, axis=0):
    return tgt.at[idx].add(src)
def _segment_sum(src, seg, n):
    return jax.ops.segment_sum(src, seg, n)

kernel_name = 'mk_adj_resnorm_d4_adj_256_4810c9'

def setup_inputs(seed: int = 0):
    np.random.seed(seed)
    _w = jnp.asarray
    def _rec_inputs():
        import jax
        import jax.numpy as jnp
        _gk = jax.random.key(seed)
        x = -0.0002928 + 1 * jax.random.normal(jax.random.fold_in(_gk, 1), (64, 256, 256), jnp.float32)
        _a = jax.random.bernoulli(jax.random.fold_in(_gk, 2), 0.125, (256, 256))
        adj = _a.astype(jnp.int32)
        return x, adj
    x, adj = _rec_inputs()
    def _L0_gnn_setup():
        import jax, jax.numpy as jnp
        import numpy as np
        ALPHA = 0.2
        NEG_INF = -1000000000000.0
        key = jax.random.key(seed)
        k1, k2, k3, k4, k5 = jax.random.split(key, 5)
        B, N, C_in, C_out = (8, 2048, 256, 256)
        inp = jax.random.normal(k1, (B, N, C_in), dtype=jnp.float32)
        adj = jax.random.randint(k2, (N, N), 0, 2, dtype=jnp.int32)
        limit = 1.414 * np.sqrt(6.0 / (C_in + C_out))
        W1 = jax.random.uniform(k3, (C_in, C_out), jnp.float32, -limit, limit)
        W2 = jax.random.uniform(k4, (C_in, C_out), jnp.float32, -limit, limit)
        W3 = jax.random.uniform(k5, (C_in, C_out), jnp.float32, -limit, limit)
        return {'inp': inp, 'adj': adj, 'W1': W1, 'W2': W2, 'W3': W3}
    _L0_gnn_all = _L0_gnn_setup()
    _L0_gnn_in = {k: v for k, v in _L0_gnn_all.items() if k in ('W1', 'W2', 'W3', )}
    del _L0_gnn_all

    def _L1_gnn_setup():
        import jax, jax.numpy as jnp
        import numpy as np
        NEG_BIG = -9000000000000000.0
        key = jax.random.key(seed)
        k1, k2, k3, k4 = jax.random.split(key, 4)
        bs, N, Fin, Fout = (8, 2048, 256, 256)
        x = jax.random.normal(k1, (bs, N, Fin), dtype=jnp.float32)
        adj = jax.random.randint(k2, (N, N), 0, 2, dtype=jnp.int32)
        W = jax.random.normal(k3, (Fin, Fout), dtype=jnp.float32) * (1.414 / np.sqrt(Fin))
        a = jax.random.normal(k4, (2 * Fout, 1), dtype=jnp.float32) * 0.1
        return {'x': x, 'adj': adj, 'W': W, 'a': a}
    _L1_gnn_all = _L1_gnn_setup()
    _L1_gnn_in = {k: v for k, v in _L1_gnn_all.items() if k in ('W', 'a', )}
    del _L1_gnn_all

    def _L2_gnn_setup():
        import jax, jax.numpy as jnp
        import numpy as np
        ALPHA = 0.2
        NEG_INF = -9000000000000000.0

        def _gat(inp, adj_mask, W, a):
            h = jnp.matmul(inp, W)
            F_ = h.shape[-1]
            f1 = jnp.matmul(h, a[:F_, 0])
            f2 = jnp.matmul(h, a[F_:, 0])
            e = jax.nn.leaky_relu(f1[:, :, None] + f2[:, None, :], ALPHA)
            if adj_mask is not None:
                e = jnp.where(adj_mask[None, :, :] > 0, e, NEG_INF)
            att = jax.nn.softmax(e, axis=2)
            h_prime = jnp.einsum('bij,bjf->bif', att, h)
            return jax.nn.elu(h_prime)
        key = jax.random.key(seed)
        ks = jax.random.split(key, 10)
        B, N, Fin, H, O = (16, 1024, 256, 512, 256)

        def xavier(k, shape):
            fan_in, fan_out = (shape[0], shape[-1])
            bound = 1.414 * np.sqrt(6.0 / (fan_in + fan_out))
            return jax.random.uniform(k, shape, jnp.float32, -bound, bound)
        return {'x': jax.random.normal(ks[0], (B, N, Fin), jnp.float32), 'adj': jax.random.randint(ks[1], (N, N), 0, 2, jnp.int32), 'mlp1_w': xavier(ks[2], (Fin, H)), 'mlp1_b': jnp.zeros((H,), jnp.float32), 'mlp2_w': xavier(ks[3], (H, O)), 'mlp2_b': jnp.zeros((O,), jnp.float32), 'W_fc': xavier(ks[4], (H, H)), 'a_fc': xavier(ks[5], (2 * H, 1)), 'W_hand': xavier(ks[6], (O, O)), 'a_hand': xavier(ks[7], (2 * O, 1))}
    _L2_gnn_all = _L2_gnn_setup()
    _L2_gnn_in = {k: v for k, v in _L2_gnn_all.items() if k in ('mlp1_w', 'mlp1_b', 'mlp2_w', 'mlp2_b', 'W_fc', 'a_fc', 'W_hand', 'a_hand', )}
    del _L2_gnn_all

    def _L3_gnn_setup():
        import jax, jax.numpy as jnp
        import numpy as np
        B, N, D_IN, D_OUT, H = (64, 512, 256, 256, 4)
        HD = D_OUT // H
        key = jax.random.key(seed)
        ks = jax.random.split(key, 10)
        x = jax.random.normal(ks[0], (B, N, D_IN), dtype=jnp.float32)
        adj = jax.random.randint(ks[1], (N, N), 0, 2, dtype=jnp.int32)
        adj = adj.at[jnp.arange(N), jnp.arange(N)].set(1)
        s_in = 1.0 / np.sqrt(D_IN)
        s_out = 1.0 / np.sqrt(D_OUT)
        wq = jax.random.uniform(ks[2], (D_OUT, D_IN), jnp.float32, -s_in, s_in)
        bq = jax.random.uniform(ks[3], (D_OUT,), jnp.float32, -s_in, s_in)
        wk = jax.random.uniform(ks[4], (D_OUT, D_IN), jnp.float32, -s_in, s_in)
        bk = jax.random.uniform(ks[5], (D_OUT,), jnp.float32, -s_in, s_in)
        wv = jax.random.uniform(ks[6], (D_OUT, D_IN), jnp.float32, -s_in, s_in)
        bv = jax.random.uniform(ks[7], (D_OUT,), jnp.float32, -s_in, s_in)
        wo = jax.random.uniform(ks[8], (D_OUT, D_OUT), jnp.float32, -s_out, s_out)
        bo = jax.random.uniform(ks[9], (D_OUT,), jnp.float32, -s_out, s_out)
        return {'x': x, 'adj': adj, 'wq': wq, 'bq': bq, 'wk': wk, 'bk': bk, 'wv': wv, 'bv': bv, 'wo': wo, 'bo': bo}
    _L3_gnn_all = _L3_gnn_setup()
    _L3_gnn_in = {k: v for k, v in _L3_gnn_all.items() if k in ('wq', 'bq', 'wk', 'bk', 'wv', 'bv', 'wo', 'bo', )}
    del _L3_gnn_all

    return {
        "x": x,
        "adj": adj,
        "L0_gnn_W1": _L0_gnn_in["W1"],
        "L0_gnn_W2": _L0_gnn_in["W2"],
        "L0_gnn_W3": _L0_gnn_in["W3"],
        "L1_gnn_W": _L1_gnn_in["W"],
        "L1_gnn_a": _L1_gnn_in["a"],
        "L2_gnn_mlp1_w": _L2_gnn_in["mlp1_w"],
        "L2_gnn_mlp1_b": _L2_gnn_in["mlp1_b"],
        "L2_gnn_mlp2_w": _L2_gnn_in["mlp2_w"],
        "L2_gnn_mlp2_b": _L2_gnn_in["mlp2_b"],
        "L2_gnn_W_fc": _L2_gnn_in["W_fc"],
        "L2_gnn_a_fc": _L2_gnn_in["a_fc"],
        "L2_gnn_W_hand": _L2_gnn_in["W_hand"],
        "L2_gnn_a_hand": _L2_gnn_in["a_hand"],
        "L3_gnn_wq": _L3_gnn_in["wq"],
        "L3_gnn_bq": _L3_gnn_in["bq"],
        "L3_gnn_wk": _L3_gnn_in["wk"],
        "L3_gnn_bk": _L3_gnn_in["bk"],
        "L3_gnn_wv": _L3_gnn_in["wv"],
        "L3_gnn_bv": _L3_gnn_in["bv"],
        "L3_gnn_wo": _L3_gnn_in["wo"],
        "L3_gnn_bo": _L3_gnn_in["bo"],
    }

def reference(x, adj, L0_gnn_W1, L0_gnn_W2, L0_gnn_W3, L1_gnn_W, L1_gnn_a, L2_gnn_mlp1_w, L2_gnn_mlp1_b, L2_gnn_mlp2_w, L2_gnn_mlp2_b, L2_gnn_W_fc, L2_gnn_a_fc, L2_gnn_W_hand, L2_gnn_a_hand, L3_gnn_wq, L3_gnn_bq, L3_gnn_wk, L3_gnn_bk, L3_gnn_wv, L3_gnn_bv, L3_gnn_wo, L3_gnn_bo):
    import jax
    import jax.numpy as jnp
    def _L0_gnn_ref(inp, adj, W1, W2, W3):
        import jax, jax.numpy as jnp
        import numpy as np
        ALPHA = 0.2
        NEG_INF = -1000000000000.0
        h1 = jnp.einsum('bnc,cd->bnd', inp, W1)
        h2 = jnp.einsum('bnc,cd->bnd', inp, W2)
        h3 = jnp.einsum('bnc,cd->bnd', inp, W3)
        e = jnp.einsum('bnd,bmd->bnm', h1, h2)
        e = jax.nn.leaky_relu(e, ALPHA)
        e = jnp.where(adj[None, :, :] > 0, e, NEG_INF)
        attention = jax.nn.softmax(e, axis=-1)
        h_prime = jnp.einsum('bnm,bmd->bnd', attention, h3)
        return jax.nn.relu(h_prime)

    def _L1_gnn_ref(x, adj, W, a):
        import jax, jax.numpy as jnp
        import numpy as np
        NEG_BIG = -9000000000000000.0
        alpha = 0.2
        h = jnp.matmul(x, W)
        Fout = h.shape[-1]
        a1, a2 = (a[:Fout, 0], a[Fout:, 0])
        s1 = jnp.einsum('bnf,f->bn', h, a1)
        s2 = jnp.einsum('bnf,f->bn', h, a2)
        e = jax.nn.leaky_relu(s1[:, :, None] + s2[:, None, :], negative_slope=alpha)
        attention = jnp.where(adj[None, :, :] > 0, e, NEG_BIG)
        attention = jax.nn.softmax(attention, axis=-1)
        h_prime = jnp.matmul(attention, h)
        return jax.nn.elu(h_prime)

    def _L2_gnn_ref(x, adj, mlp1_w, mlp1_b, mlp2_w, mlp2_b, W_fc, a_fc, W_hand, a_hand):
        import jax, jax.numpy as jnp
        import numpy as np
        ALPHA = 0.2
        NEG_INF = -9000000000000000.0

        def _gat(inp, adj_mask, W, a):
            h = jnp.matmul(inp, W)
            F_ = h.shape[-1]
            f1 = jnp.matmul(h, a[:F_, 0])
            f2 = jnp.matmul(h, a[F_:, 0])
            e = jax.nn.leaky_relu(f1[:, :, None] + f2[:, None, :], ALPHA)
            if adj_mask is not None:
                e = jnp.where(adj_mask[None, :, :] > 0, e, NEG_INF)
            att = jax.nn.softmax(e, axis=2)
            h_prime = jnp.einsum('bij,bjf->bif', att, h)
            return jax.nn.elu(h_prime)
        out = jax.nn.relu(jnp.matmul(x, mlp1_w) + mlp1_b)
        residual = out
        out = _gat(jax.nn.relu(out), None, W_fc, a_fc)
        out = jax.nn.elu(out) + residual
        out = jax.nn.relu(jnp.matmul(out, mlp2_w) + mlp2_b)
        residual = out
        out = _gat(jax.nn.relu(out), adj, W_hand, a_hand)
        out = jax.nn.elu(out) + residual
        return jax.nn.relu(out)

    def _L3_gnn_ref(x, adj, wq, bq, wk, bk, wv, bv, wo, bo):
        import jax, jax.numpy as jnp
        import numpy as np
        B, N, D_IN, D_OUT, H = (64, 512, 256, 256, 4)
        HD = D_OUT // H
        b, n, _ = x.shape
        q = (x @ wq.T + bq).reshape(b, n, H, HD).transpose(0, 2, 1, 3)
        k = (x @ wk.T + bk).reshape(b, n, H, HD).transpose(0, 2, 1, 3)
        v = (x @ wv.T + bv).reshape(b, n, H, HD).transpose(0, 2, 1, 3)
        scores = jnp.einsum('bhnd,bhmd->bhnm', q, k) / jnp.sqrt(jnp.float32(HD))
        scores = jnp.where(adj[None, None] == 0, -jnp.inf, scores)
        attn = jnp.nan_to_num(jax.nn.softmax(scores, axis=-1), nan=0.0)
        out = jnp.einsum('bhnm,bhmd->bhnd', attn, v)
        out = out.transpose(0, 2, 1, 3).reshape(b, n, D_OUT)
        return out @ wo.T + bo

    x = _layernorm(x + _L0_gnn_ref(x, adj, L0_gnn_W1, L0_gnn_W2, L0_gnn_W3), axis=-1)
    x = _layernorm(x + _L1_gnn_ref(x, adj, L1_gnn_W, L1_gnn_a), axis=-1)
    x = _layernorm(x + _L2_gnn_ref(x, adj, L2_gnn_mlp1_w, L2_gnn_mlp1_b, L2_gnn_mlp2_w, L2_gnn_mlp2_b, L2_gnn_W_fc, L2_gnn_a_fc, L2_gnn_W_hand, L2_gnn_a_hand), axis=-1)
    x = _layernorm(x + _L3_gnn_ref(x, adj, L3_gnn_wq, L3_gnn_bq, L3_gnn_wk, L3_gnn_bk, L3_gnn_wv, L3_gnn_bv, L3_gnn_wo, L3_gnn_bo), axis=-1)
    return x


_drawn_inputs = setup_inputs


def setup_inputs(seed=0):
    import zlib

    import numpy as np

    out = dict(_drawn_inputs(seed))
    spreads = {'L2_gnn_mlp1_b': (0.0, 0.1), 'L2_gnn_mlp2_b': (0.0, 0.1)}
    factors = {'L3_gnn_wq': 5.321,
     'L3_gnn_bq': 8.0,
     'L3_gnn_wk': 5.363,
     'L3_gnn_bk': 8.0,
     'L3_gnn_bv': 2.975}
    for name, (base, spread) in spreads.items():
        noise = np.random.default_rng([zlib.crc32(name.encode()), seed]).standard_normal(out[name].shape)
        drawn = base * np.exp(spread * noise) if base else spread * noise
        out[name] = jnp.asarray(drawn.astype(out[name].dtype))
    for name, factor in factors.items():
        out[name] = (out[name] * factor).astype(out[name].dtype)
    return out
```

```python
import concourse.bass as bass
from concourse import mybir
from contextlib import ExitStack

P = 128


def graph_stack(nc, x, xT, adj, ident_d, weights, out):
    fp32 = mybir.dt.float32
    bf16 = mybir.dt.bfloat16
    i32 = mybir.dt.int32
    ALU = mybir.AluOpType
    ACT = mybir.ActivationFunctionType
    AX = mybir.AxisListType

    B, N, C = out.shape
    NT = N // P
    CT = C // P
    H2 = weights["mlp1"].shape[2]
    HT = H2 // P
    HEADS = 4
    HD = C // HEADS
    MASK = -(2.0 ** 100)
    SLOPE = 0.2
    EPS = 1e-5
    QSCALE = HD ** -0.5
    STAGES = 5

    with ExitStack() as ctx:
        def sb(name, shape, dt=fp32):
            return ctx.enter_context(nc.sbuf_tensor(name, shape, dt))

        SETUP_ONLY = ("W1T", "W2T", "W_T", "hand_T", "fc_T")
        W = {n: sb("w_" + n, list(w.shape)) for n, w in weights.items() if n not in SETUP_ONLY}
        adj_sb = sb("adj_sb", [P, NT, N], i32)
        ident = sb("ident", [P, P])
        ident16 = sb("ident16", [P, P], bf16)
        ones = sb("ones", [P, P])
        zeros = sb("zeros", [P, 1, C])
        mask = sb("mask", [P, NT, N])
        mask16 = sb("mask16", [P, NT, N], bf16)
        mask3 = sb("mask3", [P, NT, N], bf16)
        some3 = sb("some3", [P, NT])
        eps = sb("eps", [P, NT])
        mhalf = sb("mhalf", [P, NT])
        A0 = sb("A0", [P, CT, C])
        v1 = sb("v1", [P, CT, 2])
        vfc = sb("vfc", [P, HT, 2])
        vha = sb("vha", [P, CT, 2])
        b2m = sb("b2m", [P, CT])
        bq8 = sb("bq8", [P, CT])

        x0T = sb("x0T", [P, CT, N])
        x0 = sb("x0", [P, NT, C])
        gT = sb("gT", [P, CT, N])
        h0 = sb("h0", [P, NT, C])
        raw = [sb(f"raw{i}", [P, NT, N]) for i in range(3)]
        sco = [sb(f"sco{i}", [P, NT, N]) for i in range(3)]
        pro = [sb(f"pro{i}", [P, NT, N]) for i in range(3)]
        proT = [sb(f"proT{i}", [P, NT, N]) for i in range(3)]
        nmax = [sb(f"nmax{i}", [P, NT]) for i in range(3)]
        den = [sb(f"den{i}", [P, NT]) for i in range(3)]
        rden = [sb(f"rden{i}", [P, NT]) for i in range(3)]
        act = [sb(f"act{i}", [P, NT, C]) for i in range(3)]
        y = [sb(f"y{i}", [P, NT, C]) for i in range(4)]
        stat = [sb(f"stat{i}", [P, NT, 6]) for i in range(4)]
        mv = [sb(f"mv{i}", [P, NT, 2]) for i in range(4)]
        vare = [sb(f"vare{i}", [P, NT]) for i in range(4)]
        rstd = [sb(f"rstd{i}", [P, NT]) for i in range(4)]
        xn = [sb(f"xn{i}", [P, NT, C]) for i in range(4)]
        xnT = [sb(f"xnT{i}", [P, CT, N]) for i in range(3)]
        h1 = sb("h1", [P, NT, C])
        f1 = sb("f1", [P, NT, 2])
        u1 = sb("u1", [P, NT, N])
        q1 = sb("q1", [P, NT, C])
        e1 = sb("e1", [P, NT, C])
        o1T = sb("o1T", [P, HT, N])
        hfc = sb("hfc", [P, NT, H2])
        ffc = sb("ffc", [P, NT, 2])
        fmax = sb("fmax", [P, 1])
        neg_pos = sb("neg_pos", [P, 2, N])
        rows = sb("rows", [P, 2, N])
        gap = sb("gap", [P, NT])
        cols = sb("cols", [P, 2, NT])
        low = sb("low", [P, NT, N])
        pfcT = sb("pfcT", [P, NT, N])
        rdb = sb("rdb", [P, N])
        att = sb("att", [P, HT, N])
        cut = sb("cut", [P, HT, N])
        ex1 = sb("ex1", [P, HT, N])
        ex2 = sb("ex2", [P, HT, N])
        res = sb("res", [P, HT, N])
        o2T = sb("o2T", [P, HT, N])
        x2b = sb("x2b", [P, NT, C])
        o3T = sb("o3T", [P, CT, N])
        h3 = sb("h3", [P, NT, C])
        f3 = sb("f3", [P, NT, 2])
        u3 = sb("u3", [P, NT, N])
        q3 = sb("q3", [P, NT, C])
        cut3 = sb("cut3", [P, NT, C])
        r3 = sb("r3", [P, NT, C])
        e3 = sb("e3", [P, NT, C])
        qT = sb("qT", [P, CT, N])
        kT = sb("kT", [P, CT, N])
        v4 = sb("v4", [P, NT, C])
        nmx4 = sb("nmx4", [P, HEADS, NT])
        p4 = sb("p4", [P, HEADS, NT, N])
        p4T = sb("p4T", [P, HEADS, NT, N])
        W.update({n: p4T[:, i, :, :] for i, n in enumerate(SETUP_ONLY[:HEADS])})
        W["fc_T"] = p4[:, :, :, :].rearrange("p h t n -> p h (t n)")
        den4 = sb("den4", [P, NT, HEADS])
        rd4 = sb("rd4", [P, NT, HEADS])
        o4 = sb("o4", [P, NT, C])
        o4T = sb("o4T", [P, CT, N])
        xb4 = sb("xb4", [P, NT, C])

        bank = [ctx.enter_context(nc.psum_tensor(f"bank{i}", [P, 2, 256], fp32)) for i in range(8)]

        names = """loaded made setup_pe setup_dve setup_pool
            x0_in x0T_in
            g0_mm g0 h0_mm h0 s0_mm raw0 sco0 nmax0 pro0 proT0_mm proT0 rden0 av0_mm act0 y0 st0 mv0 vare0 rstd0 xn0 xnT0_mm xnT0
            h1_mm h1 f1_mm f1 u1_mm u1 raw1 sco1 nmax1 pro1 proT1_mm proT1 rden1 av1_mm act1 q1 e1 y1 st1 mv1 vare1 rstd1 xn1 xnT1_mm xnT1
            o1_mm o1T ffc_mm ffc b2_mm fmax np gap rows cols low pfcT hfc0_mm hfc0 hfc1_mm hfc1 den2_mm rdb
            av2a_mm av2b_mm att_a att_b cut ex1 ex2 res o2T x2b
            o3_mm o3T h3_mm h3 f3_mm f3 u3_mm u3 raw2 sco2 nmax2 pro2 proT2_mm proT2 rden2 av3_mm o3n_mm cut3 act2 ex3 q3 r3 e3 e3b y2 st2 mv2 vare2 rstd2 xn2 xnT2_mm xnT2
            q4_mm qT k4_mm kT v4_mm v4 sc4_mm nmx4 p4 p4T_mm p4T rd4a rd4 av4_mm o4 o4T_mm o4T xb4 y4_mm y3 st3 mv3 vare3 rstd3 xn3 stored""".split()
        S = {n: ctx.enter_context(nc.semaphore("s_" + n)) for n in names}
        block = ctx.enter_context(nc.Block())

        def wait(eng, sem, n):
            if not (isinstance(n, int) and n <= 0):
                eng.wait_ge(sem, n)

        STEPS = [
            "g0 h0 s0 p0 t0 a0 n0 x0".split(),
            "h1 f1 u1 e1 p1 t1 a1 n1 x1".split(),
            "m2 f2 b2 c2 r2 w2 d2 v2 i2 y2 z2".split(),
            "m3 h3 f3 u3 e3 p3 t3 a3 z3 n3 x3".split(),
            "q4 k4 v4 s40 s41 p40 p41 t40 t41 s42 s43 p42 p43 t42 t43 a4 o4 y4 n4".split(),
        ]
        ORDER = [(s, name) for _, s, name in sorted(
            ((i + 0.5) / len(steps) * 1.0, -s, name) for s, steps in enumerate(STEPS) for i, name in enumerate(steps))]
        ORDER = [(-s, name) for s, name in ORDER]

        def run(eng, steps):
            def slot(k, active):
                for s, name in ORDER:
                    if s in active and name in steps:
                        steps[name](k - s)
            first = STAGES
            for k in range(first):
                slot(k, [s for s in range(STAGES) if 0 <= k - s])
            with eng.Fori(first, B) as k:
                slot(k, range(STAGES))
            for k in range(B, B + STAGES - 1):
                slot(k, [s for s in range(STAGES) if k - s < B])

        n_loads = len(W) + 2

        @block.sync
        def _(sp):
            for n, w in weights.items():
                sp.dma_start(W[n][:, :, :], w).then_inc(S["loaded"], 16)
            sp.dma_start(adj_sb[:, :, :], adj).then_inc(S["loaded"], 16)
            sp.dma_start(ident[:, :], ident_d).then_inc(S["loaded"], 16)

            def load_x0T(t):
                wait(sp, S["s0_mm"], t)
                sp.dma_start(x0T[:, :, :], xT[t]).then_inc(S["x0T_in"], 16)

            def load_x0(t):
                wait(sp, S["y0"], t)
                sp.dma_start(x0[:, :, :], x[t]).then_inc(S["x0_in"], 16)

            def store(t):
                wait(sp, S["xn3"], t + 1)
                sp.dma_start(out[t].rearrange("(t p) c -> p t c", p=P), xn[3][:, :, :]).then_inc(S["stored"], 16)

            run(sp, {"g0": load_x0T, "h0": load_x0, "n4": store})
            sp.wait_ge(S["stored"], 16 * B)

        @block.tensor
        def _(pe):
            def product(dst, lhs, rhs, kt, mt, first=True, last=True, off=0):
                for m in range(mt):
                    for k in range(kt):
                        ins = nc.tensor.matmul(dst[:, m, :], lhs[:, k, (off + m) * P:(off + m + 1) * P],
                                               rhs[:, k, :], start=(first and k == 0), stop=(last and k == kt - 1))
                return ins

            def transposes(dst, src):
                for a in range(2):
                    for b in range(2):
                        ins = nc.tensor.transpose(dst[:, b, a * P:(a + 1) * P], src[:, a, b * P:(b + 1) * P], ident[:, :])
                return ins

            def columns(dst, lhs, vec, kt):
                for m in range(NT):
                    for k in range(kt):
                        ins = nc.tensor.matmul(dst[:, m, 0:2], lhs[:, k, m * P:(m + 1) * P], vec[:, k, :],
                                               start=(k == 0), stop=(k == kt - 1))
                return ins

            def column_row(dst, col):
                return nc.tensor.matmul(dst, col.broadcast_to([P, P]), ident[:, :], start=True, stop=True, is_transpose=True)

            pe.wait_ge(S["loaded"], 16 * n_loads)
            product(bank[0], W["W1T"], W["W2T"], CT, CT)
            for m in range(CT):
                for k in range(CT):
                    nc.tensor.matmul(bank[1][:, m, 0:2], W["W_T"][:, k, m * P:(m + 1) * P], W["a1"][:, k, :], start=(k == 0), stop=(k == CT - 1))
                    nc.tensor.matmul(bank[2][:, m, 0:2], W["hand_T"][:, k, m * P:(m + 1) * P], W["ahand"][:, k, :], start=(k == 0), stop=(k == CT - 1))
            for m in range(HT):
                for k in range(HT):
                    nc.tensor.matmul(bank[3][:, 0, 2 * m:2 * m + 2], W["fc_T"][:, k, m * P:(m + 1) * P], W["afc"][:, k, :], start=(k == 0), stop=(k == HT - 1))
            pe.wait_ge(S["setup_pool"], 1)
            for m in range(CT):
                for k in range(HT):
                    ins = nc.tensor.matmul(bank[4][:, 0, m:m + 1], W["mlp2"][:, k, m * P:(m + 1) * P], ones[:, 0:1], start=(k == 0), stop=(k == HT - 1))
            ins.then_inc(S["setup_pe"], 1)
            pe.wait_ge(S["made"], 1)

            def g0(t):
                pe.wait_ge(S["x0T_in"], 16 * (t + 1))
                wait(pe, S["xnT0"], t)
                product(bank[0], A0, x0T, CT, CT).then_inc(S["g0_mm"], 1)

            def h0_(t):
                pe.wait_ge(S["g0"], t + 1)
                product(bank[0], x0T, W["W3"], CT, NT).then_inc(S["h0_mm"], 1)

            def s0(t):
                pe.wait_ge(S["h0"], t + 1)
                for m in range(NT):
                    nc.tensor.matmul(bank[0][:, m, :], ident16[:, :], mask16[:, m, :], start=True, stop=False)
                    for k in range(CT):
                        ins = nc.tensor.matmul(bank[0][:, m, :], gT[:, k, m * P:(m + 1) * P], x0T[:, k, :], start=False, stop=(k == CT - 1))
                ins.then_inc(S["s0_mm"], 1)

            def t0(t):
                pe.wait_ge(S["pro0"], t + 1)
                transposes(bank[0], pro[0]).then_inc(S["proT0_mm"], 1)

            def a0(t):
                pe.wait_ge(S["proT0"], t + 1)
                product(bank[0], proT[0], h0, NT, NT).then_inc(S["av0_mm"], 1)

            def x0_(t):
                pe.wait_ge(S["xn0"], t + 1)
                transposes(bank[0], xn[0]).then_inc(S["xnT0_mm"], 1)

            def h1_(t):
                pe.wait_ge(S["xnT0"], t + 1)
                wait(pe, S["xnT1"], t)
                product(bank[1], xnT[0], W["W_"], CT, NT).then_inc(S["h1_mm"], 1)

            def f1_(t):
                pe.wait_ge(S["h1"], t + 1)
                columns(bank[1], xnT[0], v1, CT).then_inc(S["f1_mm"], 1)

            def u1_(t):
                pe.wait_ge(S["f1"], t + 1)
                column_row(bank[1][:, 0, 0:P], f1[:, 0, 1:2])
                column_row(bank[1][:, 0, P:2 * P], f1[:, 1, 1:2]).then_inc(S["u1_mm"], 1)

            def t1(t):
                pe.wait_ge(S["pro1"], t + 1)
                transposes(bank[1], pro[1]).then_inc(S["proT1_mm"], 1)

            def a1(t):
                pe.wait_ge(S["proT1"], t + 1)
                product(bank[1], proT[1], h1, NT, NT).then_inc(S["av1_mm"], 1)

            def x1_(t):
                pe.wait_ge(S["xn1"], t + 1)
                transposes(bank[1], xn[1]).then_inc(S["xnT1_mm"], 1)

            def m2(t):
                pe.wait_ge(S["xnT1"], t + 1)
                wait(pe, S["att_b"], t)
                product(bank[2], W["mlp1"], xnT[1], CT, 2)
                product(bank[3], W["mlp1"], xnT[1], CT, 2, off=2).then_inc(S["o1_mm"], 1)

            def f2(t):
                pe.wait_ge(S["o1T"], t + 1)
                columns(bank[2], o1T, vfc, HT).then_inc(S["ffc_mm"], 1)

            def b2(t):
                pe.wait_ge(S["ffc"], t + 1)
                for c in range(2):
                    for m in range(NT):
                        ins = column_row(bank[2][:, c, m * P:(m + 1) * P], ffc[:, m, c:c + 1])
                ins.then_inc(S["b2_mm"], 1)

            def hidden(m, dst):
                for k in range(HT):
                    ins = nc.tensor.matmul(dst[:, :, :], o1T[:, k, m * P:(m + 1) * P], W["fc"][:, k, :], start=(k == 0), stop=(k == HT - 1))
                return ins

            def c2(t):
                hidden(0, bank[3]).then_inc(S["hfc0_mm"], 1)

            def r2(t):
                pe.wait_ge(S["hfc0"], t + 1)
                hidden(1, bank[3]).then_inc(S["hfc1_mm"], 1)

            def d2(t):
                pe.wait_ge(S["pfcT"], t + 1)
                for k in range(NT):
                    ins = nc.tensor.matmul(bank[2][:, 0, :], ones[:, :], pfcT[:, k, :], start=(k == 0), stop=(k == NT - 1))
                ins.then_inc(S["den2_mm"], 1)

            def v2(t):
                pe.wait_ge(S["hfc1"], t + 1)
                product(bank[3], hfc, pfcT, NT, 2).then_inc(S["av2a_mm"], 1)
                pe.wait_ge(S["rdb"], t + 1)
                product(bank[2], hfc, pfcT, NT, 2, off=2).then_inc(S["av2b_mm"], 1)

            def m3(t):
                pe.wait_ge(S["o2T"], t + 1)
                wait(pe, S["xnT2"], t)
                product(bank[4], W["mlp2"], o2T, HT, CT).then_inc(S["o3_mm"], 1)

            def h3_(t):
                pe.wait_ge(S["o3T"], t + 1)
                wait(pe, S["e3"], t)
                product(bank[5], o3T, W["hand"], CT, NT).then_inc(S["h3_mm"], 1)

            def f3_(t):
                columns(bank[4], o3T, vha, CT).then_inc(S["f3_mm"], 1)

            def u3_(t):
                pe.wait_ge(S["f3"], t + 1)
                column_row(bank[4][:, 0, 0:P], f3[:, 0, 1:2])
                column_row(bank[4][:, 0, P:2 * P], f3[:, 1, 1:2]).then_inc(S["u3_mm"], 1)

            def t3(t):
                pe.wait_ge(S["pro2"], t + 1)
                transposes(bank[4], pro[2]).then_inc(S["proT2_mm"], 1)

            def a3(t):
                pe.wait_ge(S["h3"], t + 1)
                transposes(bank[5], o3T).then_inc(S["o3n_mm"], 1)
                pe.wait_ge(S["proT2"], t + 1)
                product(bank[4], proT[2], h3, NT, NT).then_inc(S["av3_mm"], 1)

            def x3_(t):
                pe.wait_ge(S["xn2"], t + 1)
                transposes(bank[4], xn[2]).then_inc(S["xnT2_mm"], 1)

            def q4(t):
                pe.wait_ge(S["xnT2"], t + 1)
                wait(pe, S["y3"], t)
                product(bank[6], W["wqT"], xnT[2], CT, CT).then_inc(S["q4_mm"], 1)

            def k4(t):
                wait(pe, S["o4T"], t)
                product(bank[7], W["wkT"], xnT[2], CT, CT).then_inc(S["k4_mm"], 1)

            def v4_(t):
                pe.wait_ge(S["qT"], t + 1)
                product(bank[6], xnT[2], W["wvT"], CT, NT).then_inc(S["v4_mm"], 1)

            def scores(h):
                b = bank[7 - h % 2]
                rows_ = slice((h % 2) * HD, (h % 2) * HD + HD)
                for m in range(NT):
                    nc.tensor.matmul(b[:, m, :], ident16[:, :], mask3[:, m, :], start=True, stop=False)
                    ins = nc.tensor.matmul(b[:, m, :], qT[rows_, h // 2, m * P:(m + 1) * P], kT[rows_, h // 2, :], start=False, stop=True)
                ins.then_inc(S["sc4_mm"], 1)

            def s40(t):
                pe.wait_ge(S["kT"], t + 1)
                scores(0)

            def s41(t):
                pe.wait_ge(S["v4"], t + 1)
                scores(1)

            def s42(t):
                pe.wait_ge(S["p4T"], HEADS * t + 1)
                scores(2)

            def s43(t):
                pe.wait_ge(S["p4T"], HEADS * t + 2)
                scores(3)

            def t4(h):
                def step(t):
                    pe.wait_ge(S["p4"], HEADS * t + h + 1)
                    transposes(bank[7 - h % 2], p4[:, h, :, :]).then_inc(S["p4T_mm"], 1)
                return step

            def a4(t):
                pe.wait_ge(S["p4T"], HEADS * t + HEADS)
                for h in range(HEADS):
                    for m in range(NT):
                        for k in range(NT):
                            ins = nc.tensor.matmul(bank[6][:, m, h * HD:(h + 1) * HD], p4T[:, h, k, m * P:(m + 1) * P],
                                                   v4[:, k, h * HD:(h + 1) * HD], start=(k == 0), stop=(k == NT - 1))
                ins.then_inc(S["av4_mm"], 1)

            def o4_(t):
                pe.wait_ge(S["o4"], t + 1)
                transposes(bank[7], o4).then_inc(S["o4T_mm"], 1)

            def y4(t):
                pe.wait_ge(S["o4T"], t + 1)
                product(bank[6], o4T, W["woT"], CT, NT).then_inc(S["y4_mm"], 1)

            run(pe, {"g0": g0, "h0": h0_, "s0": s0, "t0": t0, "a0": a0, "x0": x0_,
                     "h1": h1_, "f1": f1_, "u1": u1_, "t1": t1, "a1": a1, "x1": x1_,
                     "m2": m2, "f2": f2, "b2": b2, "c2": c2, "r2": r2, "d2": d2, "v2": v2,
                     "m3": m3, "h3": h3_, "f3": f3_, "u3": u3_, "t3": t3, "a3": a3, "x3": x3_,
                     "q4": q4, "k4": k4, "v4": v4_, "s40": s40, "s41": s41, "s42": s42, "s43": s43,
                     "t40": t4(0), "t41": t4(1), "t42": t4(2), "t43": t4(3), "a4": a4, "o4": o4_, "y4": y4})

        @block.scalar
        def _(ac):
            def copy(dst, src):
                return nc.scalar.activation(dst, src, ACT.Copy)

            def exps(i):
                for m in range(NT):
                    ins = nc.scalar.activation(pro[i][:, m, :], sco[i][:, m, :], ACT.Exp, bias=nmax[i][:, m:m + 1], accum_out=den[i][:, m:m + 1])
                return ins

            ac.wait_ge(S["made"], 1)

            def g0(t):
                ac.wait_ge(S["g0_mm"], t + 1)
                copy(gT[:, :, :], bank[0][:, :, :]).then_inc(S["g0"], 1)

            def s0(t):
                ac.wait_ge(S["s0_mm"], t + 1)
                copy(raw[0][:, :, :], bank[0][:, :, :]).then_inc(S["raw0"], 1)

            def p0(t):
                ac.wait_ge(S["nmax0"], t + 1)
                exps(0).then_inc(S["pro0"], 1)

            def t0(t):
                ac.wait_ge(S["proT0_mm"], t + 1)
                copy(proT[0][:, :, :], bank[0][:, :, :]).then_inc(S["proT0"], 1)

            def a0(t):
                ac.wait_ge(S["av0_mm"], t + 1)
                ac.wait_ge(S["rden0"], t + 1)
                for m in range(NT):
                    ins = nc.scalar.activation(act[0][:, m, :], bank[0][:, m, :], ACT.Relu, scale=rden[0][:, m:m + 1])
                ins.then_inc(S["act0"], 1)

            def x0_(t):
                ac.wait_ge(S["xnT0_mm"], t + 1)
                copy(xnT[0][:, :, :], bank[0][:, :, :]).then_inc(S["xnT0"], 1)

            def u1_(t):
                ac.wait_ge(S["u1_mm"], t + 1)
                for m in range(NT):
                    ins = nc.scalar.activation(u1[:, m, :], bank[1][:, 0, :], ACT.Identity, bias=f1[:, m, 0:1])
                ins.then_inc(S["u1"], 1)

            def p1(t):
                ac.wait_ge(S["nmax1"], t + 1)
                exps(1).then_inc(S["pro1"], 1)

            def t1(t):
                ac.wait_ge(S["proT1_mm"], t + 1)
                copy(proT[1][:, :, :], bank[1][:, :, :]).then_inc(S["proT1"], 1)

            def a1(t):
                ac.wait_ge(S["av1_mm"], t + 1)
                ac.wait_ge(S["rden1"], t + 1)
                for m in range(NT):
                    ins = nc.scalar.activation(act[1][:, m, :], bank[1][:, m, :], ACT.Exp, scale=rden[1][:, m:m + 1])
                ins.then_inc(S["act1"], 1)

            def x1_(t):
                ac.wait_ge(S["xnT1_mm"], t + 1)
                copy(xnT[1][:, :, :], bank[1][:, :, :]).then_inc(S["xnT1"], 1)

            def m2(t):
                ac.wait_ge(S["o1_mm"], t + 1)
                for m in range(HT):
                    ins = nc.scalar.activation(o1T[:, m, :], bank[2 + m // 2][:, m % 2, :], ACT.Relu, bias=W["b1"][:, m, 0:1])
                ins.then_inc(S["o1T"], 1)

            def c2(t):
                ac.wait_ge(S["hfc0_mm"], t + 1)
                copy(hfc[:, 0, :].rearrange("p (a b) -> p a b", a=2), bank[3][:, :, :]).then_inc(S["hfc0"], 1)

            def r2(t):
                ac.wait_ge(S["np"], t + 1)
                nc.scalar.activation(rows[:, 0, :], neg_pos[:, 0, :], ACT.Exp, scale=1.0 - SLOPE)
                nc.scalar.activation(rows[:, 1, :], neg_pos[:, 1, :], ACT.Exp, scale=-(1.0 - SLOPE)).then_inc(S["rows"], 1)
                ac.wait_ge(S["gap"], t + 1)
                nc.scalar.activation(cols[:, 0, :], gap[:, :], ACT.Exp)
                nc.scalar.activation(cols[:, 1, :], gap[:, :], ACT.Exp, scale=SLOPE).then_inc(S["cols"], 1)
                ac.wait_ge(S["hfc1_mm"], t + 1)
                copy(hfc[:, 1, :].rearrange("p (a b) -> p a b", a=2), bank[3][:, :, :]).then_inc(S["hfc1"], 1)

            def y2(t):
                ac.wait_ge(S["cut"], t + 1)
                nc.scalar.activation(ex1[:, :, :], cut[:, :, :], ACT.Exp).then_inc(S["ex1"], 1)
                ac.wait_ge(S["ex1"], t + 1)
                nc.scalar.activation(ex2[:, :, :], ex1[:, :, :], ACT.Exp, bias=W["m1"][:, 0, 0:1]).then_inc(S["ex2"], 1)

            def m3(t):
                ac.wait_ge(S["o3_mm"], t + 1)
                for m in range(CT):
                    ins = nc.scalar.activation(o3T[:, m, :], bank[4][:, m, :], ACT.Relu, bias=b2m[:, m:m + 1])
                ins.then_inc(S["o3T"], 1)

            def u3_(t):
                ac.wait_ge(S["u3_mm"], t + 1)
                for m in range(NT):
                    ins = nc.scalar.activation(u3[:, m, :], bank[4][:, 0, :], ACT.Identity, bias=f3[:, m, 0:1])
                ins.then_inc(S["u3"], 1)

            def p3(t):
                ac.wait_ge(S["nmax2"], t + 1)
                exps(2).then_inc(S["pro2"], 1)

            def t3(t):
                ac.wait_ge(S["proT2_mm"], t + 1)
                copy(proT[2][:, :, :], bank[4][:, :, :]).then_inc(S["proT2"], 1)

            def a3(t):
                ac.wait_ge(S["cut3"], t + 1)
                nc.scalar.activation(act[2][:, :, :], cut3[:, :, :], ACT.Exp).then_inc(S["act2"], 1)
                ac.wait_ge(S["act2"], t + 1)
                nc.scalar.activation(act[2][:, :, :], act[2][:, :, :], ACT.Exp, bias=W["m1"][:, 0, 0:1]).then_inc(S["ex3"], 1)

            def x3_(t):
                ac.wait_ge(S["xnT2_mm"], t + 1)
                copy(xnT[2][:, :, :], bank[4][:, :, :]).then_inc(S["xnT2"], 1)

            def q4(t):
                ac.wait_ge(S["q4_mm"], t + 1)
                for m in range(CT):
                    ins = nc.scalar.activation(qT[:, m, :], bank[6][:, m, :], ACT.Identity, bias=bq8[:, m:m + 1], scale=QSCALE)
                ins.then_inc(S["qT"], 1)

            def k4(t):
                ac.wait_ge(S["k4_mm"], t + 1)
                for m in range(CT):
                    ins = nc.scalar.activation(kT[:, m, :], bank[7][:, m, :], ACT.Identity, bias=W["bk"][:, m, 0:1])
                ins.then_inc(S["kT"], 1)

            def p4_(h):
                def step(t):
                    ac.wait_ge(S["nmx4"], HEADS * t + h + 1)
                    for m in range(NT):
                        ins = nc.scalar.activation(p4[:, h, m, :], bank[7 - h % 2][:, m, :], ACT.Exp,
                                                   bias=nmx4[:, h, m:m + 1], accum_out=den4[:, m, h:h + 1])
                    ins.then_inc(S["p4"], 1)
                return step

            def t4(h):
                def step(t):
                    ac.wait_ge(S["p4T_mm"], HEADS * t + h + 1)
                    copy(p4T[:, h, :, :], bank[7 - h % 2][:, :, :]).then_inc(S["p4T"], 1)
                return step

            def o4_(t):
                ac.wait_ge(S["o4T_mm"], t + 1)
                copy(o4T[:, :, :], bank[7][:, :, :]).then_inc(S["o4T"], 1)

            run(ac, {"g0": g0, "s0": s0, "p0": p0, "t0": t0, "a0": a0, "x0": x0_,
                     "u1": u1_, "p1": p1, "t1": t1, "a1": a1, "x1": x1_,
                     "m2": m2, "c2": c2, "r2": r2, "y2": y2,
                     "m3": m3, "u3": u3_, "p3": p3, "t3": t3, "a3": a3, "x3": x3_,
                     "q4": q4, "k4": k4, "p40": p4_(0), "p41": p4_(1), "p42": p4_(2), "p43": p4_(3),
                     "t40": t4(0), "t41": t4(1), "t42": t4(2), "t43": t4(3), "o4": o4_})

        @block.vector
        def _(dv):
            V = nc.vector
            dv.wait_ge(S["loaded"], 16 * n_loads)
            V.tensor_copy(ident16[:, :], ident[:, :])
            V.tensor_scalar(mask[:, :, :], adj_sb[:, :, :], 0.0, MASK, ALU.is_le, ALU.mult)
            V.tensor_scalar(mask16[:, :, :], adj_sb[:, :, :], 0.0, MASK, ALU.is_le, ALU.mult)
            V.tensor_scalar(mask3[:, :, :], adj_sb[:, :, :], 0.0, MASK, ALU.is_equal, ALU.mult).then_inc(S["setup_dve"], 1)
            dv.wait_ge(S["setup_dve"], 1)
            V.reduce_max(some3[:, :], mask3[:, :, :], AX.X).then_inc(S["setup_dve"], 1)
            dv.wait_ge(S["setup_dve"], 2)
            V.tensor_scalar(some3[:, :], some3[:, :], 0.0, None, ALU.is_equal)
            V.tensor_scalar(bq8[:, :], W["bq"][:, :, 0], QSCALE, None, ALU.mult)
            dv.wait_ge(S["setup_pe"], 1)
            V.tensor_copy(A0[:, :, :], bank[0][:, :, :])
            V.tensor_copy(v1[:, :, :], bank[1][:, :, 0:2])
            V.tensor_copy(vha[:, :, :], bank[2][:, :, 0:2])
            V.tensor_copy(vfc[:, :, :], bank[3][:, 0, 0:2 * HT].rearrange("p (m c) -> p m c", c=2))
            V.tensor_tensor(b2m[:, :], W["b2"][:, :, 0], bank[4][:, 0, 0:CT], ALU.subtract).then_inc(S["made"], 1)

            def leaky(i, s, a, b, t):
                V.scalar_tensor_tensor(sco[i][:, :, :], a, SLOPE, b, ALU.mult, ALU.max).then_inc(s[0], 1)
                dv.wait_ge(s[0], t + 1)
                V.tensor_reduce(nmax[i][:, :], sco[i][:, :, :], AX.X, ALU.max, negate=True).then_inc(s[1], 1)

            def stats(i, s_y, s_st, s_mv, t):
                dv.wait_ge(s_y, t + 1)
                for m in range(NT):
                    ins = V.bn_stats(stat[i][:, m, :], y[i][:, m, :])
                ins.then_inc(s_st, 1)
                dv.wait_ge(S["loaded"], 16)
                dv.wait_ge(s_st, t + 1)
                for m in range(NT):
                    ins = V.bn_aggr(mv[i][:, m, :], stat[i][:, m, :])
                ins.then_inc(s_mv, 1)

            def norm(i):
                for m in range(NT):
                    ins = V.tensor_scalar(xn[i][:, m, :], y[i][:, m, :], mv[i][:, m, 0:1], rstd[i][:, m:m + 1], ALU.subtract, ALU.mult)
                return ins

            def h0_(t):
                dv.wait_ge(S["h0_mm"], t + 1)
                V.tensor_copy(h0[:, :, :], bank[0][:, :, :]).then_inc(S["h0"], 1)

            def s0(t):
                dv.wait_ge(S["raw0"], t + 1)
                leaky(0, (S["sco0"], S["nmax0"]), bank[0][:, :, :], raw[0][:, :, :], t)

            def t0(t):
                dv.wait_ge(S["pro0"], t + 1)
                V.reciprocal(rden[0][:, :], den[0][:, :]).then_inc(S["rden0"], 1)

            def a0(t):
                stats(0, S["y0"], S["st0"], S["mv0"], t)

            def n0(t):
                dv.wait_ge(S["rstd0"], t + 1)
                wait(dv, S["y1"], t)
                norm(0).then_inc(S["xn0"], 1)

            def h1_(t):
                dv.wait_ge(S["h1_mm"], t + 1)
                V.tensor_copy(h1[:, :, :], bank[1][:, :, :]).then_inc(S["h1"], 1)

            def f1_(t):
                dv.wait_ge(S["f1_mm"], t + 1)
                V.tensor_copy(f1[:, :, :], bank[1][:, :, 0:2]).then_inc(S["f1"], 1)

            def e1_(t):
                dv.wait_ge(S["raw1"], t + 1)
                leaky(1, (S["sco1"], S["nmax1"]), raw[1][:, :, :], raw[1][:, :, :], t)

            def t1(t):
                dv.wait_ge(S["pro1"], t + 1)
                V.reciprocal(rden[1][:, :], den[1][:, :]).then_inc(S["rden1"], 1)

            def a1(t):
                dv.wait_ge(S["act1"], t + 1)
                for m in range(NT):
                    ins = V.tensor_scalar(q1[:, m, :], bank[1][:, m, :], rden[1][:, m:m + 1], 0.0, ALU.mult, ALU.max)
                ins.then_inc(S["q1"], 1)
                dv.wait_ge(S["q1"], t + 1)
                V.scalar_tensor_tensor(e1[:, :, :], act[1][:, :, :], 1.0, q1[:, :, :], ALU.min, ALU.add).then_inc(S["e1"], 1)
                stats(1, S["y1"], S["st1"], S["mv1"], t)

            def n1(t):
                dv.wait_ge(S["rstd1"], t + 1)
                wait(dv, S["x2b"], t)
                norm(1).then_inc(S["xn1"], 1)

            def f2(t):
                dv.wait_ge(S["ffc_mm"], t + 1)
                V.tensor_copy(ffc[:, :, :], bank[2][:, :, 0:2]).then_inc(S["ffc"], 1)

            def b2(t):
                dv.wait_ge(S["b2_mm"], t + 1)
                V.reduce_max(fmax[:, :], bank[2][:, 1, :], AX.X).then_inc(S["fmax"], 1)
                dv.wait_ge(S["fmax"], t + 1)
                V.tensor_scalar(neg_pos[:, 0, :], bank[2][:, 0, :], fmax[:, 0:1], 0.0, ALU.add, ALU.min)
                V.tensor_scalar(neg_pos[:, 1, :], bank[2][:, 0, :], fmax[:, 0:1], 0.0, ALU.add, ALU.max).then_inc(S["np"], 1)
                V.tensor_scalar(gap[:, :], ffc[:, :, 1], fmax[:, 0:1], None, ALU.subtract).then_inc(S["gap"], 1)

            def w2(t):
                dv.wait_ge(S["rows"], t + 1)
                dv.wait_ge(S["cols"], t + 1)
                for m in range(NT):
                    ins = V.tensor_scalar(low[:, m, :], rows[:, 1, :], cols[:, 1, m:m + 1], None, ALU.mult)
                ins.then_inc(S["low"], 1)
                dv.wait_ge(S["low"], t + 1)
                for m in range(NT):
                    ins = V.scalar_tensor_tensor(pfcT[:, m, :], rows[:, 0, :], cols[:, 0, m:m + 1], low[:, m, :], ALU.mult, ALU.max)
                ins.then_inc(S["pfcT"], 1)

            def v2(t):
                dv.wait_ge(S["den2_mm"], t + 1)
                V.reciprocal(rdb[:, :], bank[2][:, 0, :]).then_inc(S["rdb"], 1)
                dv.wait_ge(S["rdb"], t + 1)
                rb = rdb[:, :].unsqueeze(1).broadcast_to([P, 2, N])
                dv.wait_ge(S["av2a_mm"], t + 1)
                V.tensor_tensor(att[:, 0:2, :], bank[3][:, :, :], rb, ALU.mult).then_inc(S["att_a"], 1)
                dv.wait_ge(S["av2b_mm"], t + 1)
                V.tensor_tensor(att[:, 2:4, :], bank[2][:, :, :], rb, ALU.mult).then_inc(S["att_b"], 1)

            def i2(t):
                dv.wait_ge(S["att_b"], t + 1)
                V.tensor_scalar(cut[:, :, :], att[:, :, :], 0.0, None, ALU.min).then_inc(S["cut"], 1)
                V.scalar_tensor_tensor(res[:, :, :], att[:, :, :], 0.0, o1T[:, :, :], ALU.max, ALU.add).then_inc(S["res"], 1)

            def h3_(t):
                dv.wait_ge(S["h3_mm"], t + 1)
                V.tensor_copy(h3[:, :, :], bank[5][:, :, :]).then_inc(S["h3"], 1)

            def f3_(t):
                dv.wait_ge(S["f3_mm"], t + 1)
                V.tensor_copy(f3[:, :, :], bank[4][:, :, 0:2]).then_inc(S["f3"], 1)

            def e3_(t):
                dv.wait_ge(S["raw2"], t + 1)
                leaky(2, (S["sco2"], S["nmax2"]), raw[2][:, :, :], raw[2][:, :, :], t)

            def t3(t):
                dv.wait_ge(S["pro2"], t + 1)
                V.reciprocal(rden[2][:, :], den[2][:, :]).then_inc(S["rden2"], 1)

            def a3(t):
                dv.wait_ge(S["rden2"], t + 1)
                dv.wait_ge(S["av3_mm"], t + 1)
                for m in range(NT):
                    ins = V.tensor_scalar(cut3[:, m, :], bank[4][:, m, :], rden[2][:, m:m + 1], 0.0, ALU.mult, ALU.min)
                ins.then_inc(S["cut3"], 1)
                for m in range(NT):
                    ins = V.tensor_scalar(q3[:, m, :], bank[4][:, m, :], rden[2][:, m:m + 1], 0.0, ALU.mult, ALU.max)
                ins.then_inc(S["q3"], 1)
                dv.wait_ge(S["q3"], t + 1)
                dv.wait_ge(S["o3n_mm"], t + 1)
                V.scalar_tensor_tensor(r3[:, :, :], q3[:, :, :], -1.0, bank[5][:, :, :], ALU.add, ALU.add).then_inc(S["r3"], 1)

            def z3(t):
                dv.wait_ge(S["e3"], t + 1)
                dv.wait_ge(S["x2b"], t + 1)
                V.scalar_tensor_tensor(y[2][:, :, :], e3[:, :, :], 0.0, x2b[:, :, :], ALU.max, ALU.add).then_inc(S["y2"], 1)
                stats(2, S["y2"], S["st2"], S["mv2"], t)

            def n3(t):
                dv.wait_ge(S["rstd2"], t + 1)
                wait(dv, S["xb4"], t)
                norm(2).then_inc(S["xn2"], 1)

            def v4_(t):
                dv.wait_ge(S["v4_mm"], t + 1)
                V.tensor_tensor(v4[:, :, :], bank[6][:, :, :], W["bv"][:, 0:1, :].broadcast_to([P, NT, C]), ALU.add).then_inc(S["v4"], 1)

            def s4(h):
                def step(t):
                    dv.wait_ge(S["sc4_mm"], HEADS * t + h + 1)
                    V.tensor_reduce(nmx4[:, h, :], bank[7 - h % 2][:, :, :], AX.X, ALU.max, negate=True).then_inc(S["nmx4"], 1)
                return step

            def a4(t):
                dv.wait_ge(S["p4"], HEADS * t + HEADS)
                V.reciprocal(den4[:, :, :], den4[:, :, :]).then_inc(S["rd4a"], 1)
                dv.wait_ge(S["rd4a"], t + 1)
                V.tensor_tensor(rd4[:, :, :], den4[:, :, :], some3[:, :].unsqueeze(2).broadcast_to([P, NT, HEADS]), ALU.mult).then_inc(S["rd4"], 1)
                dv.wait_ge(S["rd4"], t + 1)
                dv.wait_ge(S["av4_mm"], t + 1)
                V.tensor_tensor(o4[:, :, :].rearrange("p t (h d) -> p (t h) d", h=HEADS),
                                bank[6][:, :, :].rearrange("p t (h d) -> p (t h) d", h=HEADS),
                                rd4[:, :, :].rearrange("p t h -> p (t h)").unsqueeze(2).broadcast_to([P, NT * HEADS, HD]),
                                ALU.mult).then_inc(S["o4"], 1)

            def y4(t):
                dv.wait_ge(S["y4_mm"], t + 1)
                dv.wait_ge(S["xb4"], t + 1)
                V.tensor_tensor(y[3][:, :, :], bank[6][:, :, :], xb4[:, :, :], ALU.add).then_inc(S["y3"], 1)
                stats(3, S["y3"], S["st3"], S["mv3"], t)

            def n4(t):
                dv.wait_ge(S["rstd3"], t + 1)
                wait(dv, S["stored"], 16 * t)
                norm(3).then_inc(S["xn3"], 1)

            run(dv, {"h0": h0_, "s0": s0, "t0": t0, "a0": a0, "n0": n0,
                     "h1": h1_, "f1": f1_, "e1": e1_, "t1": t1, "a1": a1, "n1": n1,
                     "f2": f2, "b2": b2, "w2": w2, "v2": v2, "i2": i2,
                     "h3": h3_, "f3": f3_, "e3": e3_, "t3": t3, "a3": a3, "z3": z3, "n3": n3,
                     "v4": v4_, "s40": s4(0), "s41": s4(1), "s42": s4(2), "s43": s4(3), "a4": a4, "y4": y4, "n4": n4})

        @block.gpsimd
        def _(po):
            G = nc.gpsimd
            G.memset(eps[:, :], EPS)
            G.memset(mhalf[:, :], -0.5)
            G.memset(zeros[:, :, :], 0.0)
            G.memset(ones[:, :], 1.0).then_inc(S["setup_pool"], 1)
            po.wait_ge(S["setup_pool"], 1)
            po.wait_ge(S["made"], 1)

            def inv_std(i, s_mv, s_ve, s_rs, t):
                po.wait_ge(s_mv, t + 1)
                G.tensor_tensor(vare[i][:, :], mv[i][:, :, 1], eps[:, :], ALU.add).then_inc(s_ve, 1)
                po.wait_ge(s_ve, t + 1)
                G.tensor_tensor(rstd[i][:, :], vare[i][:, :], mhalf[:, :], ALU.pow).then_inc(s_rs, 1)

            def a0(t):
                po.wait_ge(S["x0_in"], 16 * (t + 1))
                po.wait_ge(S["act0"], t + 1)
                G.tensor_tensor(y[0][:, :, :], act[0][:, :, :], x0[:, :, :], ALU.add).then_inc(S["y0"], 1)
                inv_std(0, S["mv0"], S["vare0"], S["rstd0"], t)

            def u1_(t):
                po.wait_ge(S["u1"], t + 1)
                G.tensor_tensor(raw[1][:, :, :], u1[:, :, :], mask[:, :, :], ALU.add).then_inc(S["raw1"], 1)

            def a1(t):
                po.wait_ge(S["e1"], t + 1)
                G.tensor_tensor(y[1][:, :, :], e1[:, :, :], xn[0][:, :, :], ALU.add).then_inc(S["y1"], 1)
                inv_std(1, S["mv1"], S["vare1"], S["rstd1"], t)

            def i2(t):
                wait(po, S["y2"], t)
                po.wait_ge(S["xn1"], t + 1)
                G.tensor_tensor(x2b[:, :, :], xn[1][:, :, :], zeros[:, :, :].broadcast_to([P, NT, C]), ALU.add).then_inc(S["x2b"], 1)

            def z2(t):
                po.wait_ge(S["ex2"], t + 1)
                po.wait_ge(S["res"], t + 1)
                wait(po, S["o3_mm"], t)
                G.tensor_tensor(o2T[:, :, :], ex2[:, :, :], res[:, :, :], ALU.add).then_inc(S["o2T"], 1)

            def u3_(t):
                po.wait_ge(S["u3"], t + 1)
                G.tensor_tensor(raw[2][:, :, :], u3[:, :, :], mask[:, :, :], ALU.add).then_inc(S["raw2"], 1)

            def a3(t):
                po.wait_ge(S["ex3"], t + 1)
                po.wait_ge(S["r3"], t + 1)
                G.tensor_tensor(e3[:, :, :], act[2][:, :, :], r3[:, :, :], ALU.add).then_inc(S["e3"], 1)

            def z3(t):
                inv_std(2, S["mv2"], S["vare2"], S["rstd2"], t)

            def k4(t):
                po.wait_ge(S["xn2"], t + 1)
                G.tensor_tensor(xb4[:, :, :], xn[2][:, :, :], W["bo"][:, 0:1, :].broadcast_to([P, NT, C]), ALU.add).then_inc(S["xb4"], 1)

            def y4(t):
                inv_std(3, S["mv3"], S["vare3"], S["rstd3"], t)

            run(po, {"a0": a0, "u1": u1_, "a1": a1, "i2": i2, "z2": z2, "u3": u3_, "a3": a3, "z3": z3, "k4": k4, "y4": y4})


def kernel(**inputs):
    import numpy as np
    import concourse.bacc as bacc
    from concourse.bass_utils import run_bass_kernel_spmd

    a = {n: np.asarray(v) for n, v in inputs.items()}
    x = a["x"]
    column = lambda v: v.reshape(-1, 1)
    spread = lambda v: np.repeat(v.reshape(1, -1), P, axis=0)
    layout = {
        "W1T": a["L0_gnn_W1"].T, "W2T": a["L0_gnn_W2"].T, "W3": a["L0_gnn_W3"],
        "W_": a["L1_gnn_W"], "W_T": a["L1_gnn_W"].T, "a1": a["L1_gnn_a"].reshape(2, -1).T,
        "mlp1": a["L2_gnn_mlp1_w"], "b1": column(a["L2_gnn_mlp1_b"]),
        "fc": a["L2_gnn_W_fc"], "fc_T": a["L2_gnn_W_fc"].T, "afc": a["L2_gnn_a_fc"].reshape(2, -1).T,
        "mlp2": a["L2_gnn_mlp2_w"], "b2": column(a["L2_gnn_mlp2_b"]),
        "hand": a["L2_gnn_W_hand"], "hand_T": a["L2_gnn_W_hand"].T, "ahand": a["L2_gnn_a_hand"].reshape(2, -1).T,
        "wqT": a["L3_gnn_wq"].T, "bq": column(a["L3_gnn_bq"]),
        "wkT": a["L3_gnn_wk"].T, "bk": column(a["L3_gnn_bk"]),
        "wvT": a["L3_gnn_wv"].T, "bv": spread(a["L3_gnn_bv"]),
        "woT": a["L3_gnn_wo"].T, "bo": spread(a["L3_gnn_bo"]),
        "m1": np.full((P, 1), -1.0, np.float32),
    }
    nc = bacc.Bacc("TRN2", target_bir_lowering=False, num_devices=1)
    arrays = {}

    def dram(name, v):
        arrays[name] = np.ascontiguousarray(v)
        return nc.dram_tensor(name, v.shape, mybir.dt.from_np(v.dtype), kind="ExternalInput").ap()

    tiled = lambda v: np.swapaxes(v.reshape(*v.shape[:-2], -1, P, v.shape[-1]), -3, -2)
    weights = {n: dram("in_" + n, tiled(v)) for n, v in layout.items()}
    ins = [dram("in_x", tiled(x)), dram("in_xT", tiled(np.transpose(x, (0, 2, 1)))), dram("in_adj", tiled(a["adj"])),
           dram("in_ident", np.eye(P, dtype=np.float32))]
    out = nc.dram_tensor("out", x.shape, mybir.dt.from_np(x.dtype), kind="ExternalOutput").ap()
    graph_stack(nc, *ins, weights, out)
    return run_bass_kernel_spmd(nc, [arrays], core_ids=[0]).results[0]["out"]
```

```python
import concourse.bass as bass
from concourse import mybir
from contextlib import ExitStack

P = 128


def graph_stack(nc, x, xT, adj, ident_d, weights, out):
    fp32 = mybir.dt.float32
    f32r = mybir.dt.float32r
    bf16 = mybir.dt.bfloat16
    i32 = mybir.dt.int32
    ALU = mybir.AluOpType
    ACT = mybir.ActivationFunctionType
    AX = mybir.AxisListType

    B, N, C = out.shape
    NT = N // P
    CT = C // P
    H2 = weights["mlp1"].shape[2]
    HT = H2 // P
    HEADS = 4
    HD = C // HEADS
    MASK = -(2.0 ** 100)
    SLOPE = 0.2
    EPS = 1e-5
    QSCALE = HD ** -0.5
    STAGES = 6

    with ExitStack() as ctx:
        def sb(name, shape, dt=fp32):
            return ctx.enter_context(nc.sbuf_tensor(name, shape, dt))

        SETUP_ONLY = ("W1T", "W2T", "W_T", "hand_T", "fc_T", "fc", "mlp1", "mlp2", "wqT", "wkT", "wvT", "W3")
        W = {n: sb("w_" + n, list(w.shape)) for n, w in weights.items() if n not in SETUP_ONLY}
        def parts(name, shape):
            return sb(name + "_hi", shape, f32r), sb(name + "_lo", shape, f32r)
        SPLIT = ("fc", "mlp1", "mlp2", "wqT", "wkT", "wvT", "W3")
        WP = {n: parts("w_" + n, list(weights[n].shape)) for n in SPLIT}
        adj_sb = sb("adj_sb", [P, NT, N], i32)
        ident = sb("ident", [P, P])
        ident16 = sb("ident16", [P, P], bf16)
        ones = sb("ones", [P, P])
        zeros = sb("zeros", [P, 1, C])
        mask = sb("mask", [P, NT, N])
        mask16 = sb("mask16", [P, NT, N], bf16)
        mask3 = sb("mask3", [P, NT, N], bf16)
        some3 = sb("some3", [P, NT])
        eps = sb("eps", [P, NT])
        mhalf = sb("mhalf", [P, NT])
        A0 = parts("A0", [P, CT, C])
        v1 = sb("v1", [P, CT, 2])
        vfc = sb("vfc", [P, HT, 2])
        vha = sb("vha", [P, CT, 2])
        b2m = sb("b2m", [P, CT])
        bq8 = sb("bq8", [P, CT])

        x0T = sb("x0T", [P, CT, N])
        x0 = sb("x0", [P, NT, C])
        x0Tp = parts("x0Tp", [P, CT, N])
        gT = parts("gT", [P, CT, N])
        h0 = sb("h0", [P, NT, C])
        sco = [sb(f"sco{i}", [P, NT, N]) for i in range(3)]
        pro = raw = sco
        proT = [sb(f"proT{i}", [P, NT, N]) for i in range(3)]
        nmax = [sb(f"nmax{i}", [P, NT]) for i in range(3)]
        den = [sb(f"den{i}", [P, NT]) for i in range(3)]
        rden = [sb(f"rden{i}", [P, NT]) for i in range(3)]
        act = [sb(f"act{i}", [P, NT, C]) for i in range(3)]
        A0f = act[1]
        y = [sb(f"y{i}", [P, NT, C]) for i in range(4)]
        stat = [sb(f"stat{i}", [P, NT, 6]) for i in range(4)]
        mv = [sb(f"mv{i}", [P, NT, 2]) for i in range(4)]
        vare = [sb(f"vare{i}", [P, NT]) for i in range(4)]
        rstd = [sb(f"rstd{i}", [P, NT]) for i in range(4)]
        xn = [sb(f"xn{i}", [P, NT, C]) for i in range(4)]
        xnT = [sb("xnT0", [P, CT, N]), parts("xnT1", [P, CT, N]), parts("xnT2", [P, CT, N])]
        h1 = sb("h1", [P, NT, C])
        f1 = sb("f1", [P, NT, 2])
        u1 = sco[1]
        q1 = e1 = y[1]
        o1T = sb("o1T", [P, HT, N])
        o1Tp = parts("o1Tp", [P, HT, N])
        hfc = sb("hfc", [P, NT, H2])
        ffc = sb("ffc", [P, NT, 2])
        fmax = sb("fmax", [P, 1])
        neg_pos = sb("neg_pos", [P, 2, N])
        rows = neg_pos
        gap = sb("gap", [P, NT])
        cols = sb("cols", [P, 2, NT])
        low = sb("low", [P, NT, N])
        pfcT = sb("pfcT", [P, NT, N])
        rdb = sb("rdb", [P, N])
        att_cut = sb("att_cut", [P, 2, HT, N])
        att, cut = att_cut[:, 0, :, :], att_cut[:, 1, :, :]
        res, ex1, ex2 = att, cut, cut
        o2 = sb("o2", [P, HT, N])
        o2T = parts("o2T", [P, HT, N])
        x2b = sb("x2b", [P, NT, C])
        o3T = sb("o3T", [P, CT, N])
        h3 = sb("h3", [P, NT, C])
        f3 = sb("f3", [P, NT, 2])
        u3 = sco[2]
        q3 = r3 = e3 = y[2]
        cut3 = act[2]
        qT = sb("qT", [P, CT, N])
        kT = sb("kT", [P, CT, N])
        v4 = sb("v4", [P, NT, C])
        nmx4 = sb("nmx4", [P, HEADS, NT])
        p4 = sb("p4", [P, HEADS, NT, N])
        p4T = sb("p4T", [P, HEADS, NT, N])
        W.update({n: p4T[:, i, :, :] for i, n in enumerate(SETUP_ONLY[:HEADS])})
        W.update({"fc": att_cut[:, :, :, :].rearrange("p a (b h) n -> p (a b) (h n)", h=2), "mlp1": hfc[:, :, :], "mlp2": o2[:, :, :],
                  "wqT": sco[0][:, :, :], "wkT": sco[1][:, :, :], "wvT": sco[2][:, :, :], "W3": act[0][:, :, :]})
        W["fc_T"] = p4[:, :, :, :].rearrange("p h t n -> p h (t n)")
        den4 = sb("den4", [P, NT, HEADS])
        rd4 = sb("rd4", [P, NT, HEADS])
        o4 = sb("o4", [P, NT, C])
        o4T = sb("o4T", [P, CT, N])
        xb4 = sb("xb4", [P, NT, C])

        bank = [ctx.enter_context(nc.psum_tensor(f"bank{i}", [P, 2, 256], fp32)) for i in range(8)]

        names = """loaded made setup_pe setup_dve setup_pool
            x0_in x0T_in x0Th x0Tl g0h xnT1h xnT2h o1Th o1Tl o2 o2Th wsplit
            g0_mm g0 h0_mm h0 s0_mm raw0 sco0 nmax0 pro0 proT0_mm proT0 rden0 av0_mm act0 y0 st0 mv0 vare0 rstd0 xn0 xnT0_mm xnT0
            h1_mm h1 f1_mm f1 u1_mm u1 raw1 sco1 nmax1 pro1 proT1_mm proT1 rden1 av1_mm act1 q1 e1 y1 st1 mv1 vare1 rstd1 xn1 xnT1_mm xnT1
            o1_mm o1T ffc_mm ffc b2_mm fmax np gap rows cols low pfcT hfc0_mm hfc0 hfc1_mm hfc1 den2_mm rdb
            av2a_mm av2b_mm att_a att_b cut ex1 ex2 res o2T x2b
            o3_mm o3T h3_mm h3 f3_mm f3 u3_mm u3 raw2 sco2 nmax2 pro2 proT2_mm proT2 rden2 av3_mm o3n_mm cut3 act2 ex3 q3 r3 e3 e3b y2 st2 mv2 vare2 rstd2 xn2 xnT2_mm xnT2
            q4_mm qT k4_mm kT v4_mm v4 sc4_mm nmx4 p4 p4T_mm p4T rd4a rd4 av4_mm o4 o4T_mm o4T xb4 y4_mm y3 st3 mv3 vare3 rstd3 xn3 stored""".split()
        S = {n: ctx.enter_context(nc.semaphore("s_" + n)) for n in names}
        block = ctx.enter_context(nc.Block())

        def wait(eng, sem, n):
            if not (isinstance(n, int) and n <= 0):
                eng.wait_ge(sem, n)

        STEPS = [
            "l0 l2 l1".split(),
            "g0 h0 s0 p0 t0 a0 n0 x0".split(),
            "h1 f1 u1 e1 p1 t1 a1 n1 x1".split(),
            "m2 f2 b2 c2 r2 w2 d2 v2 i2 y2 z2".split(),
            "m3 h3 f3 u3 e3 p3 t3 a3 z3 n3 x3".split(),
            "q4 k4 v4 s40 s41 p40 p41 t40 t41 s42 s43 p42 p43 t42 t43 a4 o4 y4 n4".split(),
        ]
        ORDER = """
            h1 g0 q4 m2 k4 m3 h0 f1 h3 u1 v4 e1 s0 p1 f3 p0 s40 s41 l0 t0 u3 p40 t1 p41 f2 e3 a0 p3 t40 a1 t41
            t3 s42 s43 p42 a3 n0 p43 b2 c2 t42 l2 t43 z3 r2 w2 a4 l1 d2 x0 o4 n1 v2 n3 x1 i2 y4 y2 x3 z2 n4
        """.split()
        ORDER = [(s, name) for name in ORDER for s, steps in enumerate(STEPS) if name in steps]
        assert len(ORDER) == sum(len(steps) for steps in STEPS)

        def run(eng, steps):
            def slot(k, active):
                for s, name in ORDER:
                    if s in active and name in steps:
                        steps[name](k - s)
            first = STAGES
            for k in range(first):
                slot(k, [s for s in range(STAGES) if 0 <= k - s])
            with eng.Fori(first, B) as k:
                slot(k, range(STAGES))
            for k in range(B, B + STAGES - 1):
                slot(k, [s for s in range(STAGES) if k - s < B])

        n_loads = len(W) + 2

        @block.sync
        def _(sp):
            for n, w in weights.items():
                sp.dma_start(W[n][:, :, :], w).then_inc(S["loaded"], 16)
            sp.dma_start(adj_sb[:, :, :], adj).then_inc(S["loaded"], 16)
            sp.dma_start(ident[:, :], ident_d).then_inc(S["loaded"], 16)

            def load_x0T(t):
                wait(sp, S["x0Tl"], t)
                sp.dma_start(x0T[:, :, :], xT[t]).then_inc(S["x0T_in"], 16)

            def load_x0(t):
                wait(sp, S["y0"], t)
                sp.dma_start(x0[:, :, :], x[t]).then_inc(S["x0_in"], 16)

            def store(t):
                wait(sp, S["xn3"], t + 1)
                sp.dma_start(out[t].rearrange("(t p) c -> p t c", p=P), xn[3][:, :, :]).then_inc(S["stored"], 16)

            run(sp, {"l0": load_x0T, "l1": load_x0, "n4": store})
            sp.wait_ge(S["stored"], 16 * B)

        @block.tensor
        def _(pe):
            def product(dst, lhs, rhs, kt, mt, first=True, last=True, off=0):
                for m in range(mt):
                    for k in range(kt):
                        ins = nc.tensor.matmul(dst[:, m, :], lhs[:, k, (off + m) * P:(off + m + 1) * P],
                                               rhs[:, k, :], start=(first and k == 0), stop=(last and k == kt - 1))
                return ins

            def product3(dst, lhs, rhs, kt, mt, first=True, off=0):
                for m in range(mt):
                    for k in range(kt):
                        for i, (a, b) in enumerate(((0, 1), (1, 0), (0, 0))):
                            ins = nc.tensor.matmul(dst[:, m, :], lhs[a][:, k, (off + m) * P:(off + m + 1) * P], rhs[b][:, k, :],
                                                   start=(first and k == 0 and i == 0), stop=(k == kt - 1 and i == 2))
                return ins

            def transposes(dst, src):
                for a in range(2):
                    for b in range(2):
                        ins = nc.tensor.transpose(dst[:, b, a * P:(a + 1) * P], src[:, a, b * P:(b + 1) * P], ident[:, :])
                return ins

            def columns(dst, lhs, vec, kt):
                for m in range(NT):
                    for k in range(kt):
                        ins = nc.tensor.matmul(dst[:, m, 0:2], lhs[:, k, m * P:(m + 1) * P], vec[:, k, :],
                                               start=(k == 0), stop=(k == kt - 1))
                return ins

            def column_row(dst, col):
                return nc.tensor.matmul(dst, col.broadcast_to([P, P]), ident[:, :], start=True, stop=True, is_transpose=True)

            pe.wait_ge(S["loaded"], 16 * n_loads)
            product(bank[0], W["W1T"], W["W2T"], CT, CT)
            for m in range(CT):
                for k in range(CT):
                    nc.tensor.matmul(bank[1][:, m, 0:2], W["W_T"][:, k, m * P:(m + 1) * P], W["a1"][:, k, :], start=(k == 0), stop=(k == CT - 1))
                    nc.tensor.matmul(bank[2][:, m, 0:2], W["hand_T"][:, k, m * P:(m + 1) * P], W["ahand"][:, k, :], start=(k == 0), stop=(k == CT - 1))
            for m in range(HT):
                for k in range(HT):
                    nc.tensor.matmul(bank[3][:, 0, 2 * m:2 * m + 2], W["fc_T"][:, k, m * P:(m + 1) * P], W["afc"][:, k, :], start=(k == 0), stop=(k == HT - 1))
            pe.wait_ge(S["setup_pool"], 1)
            for m in range(CT):
                for k in range(HT):
                    ins = nc.tensor.matmul(bank[4][:, 0, m:m + 1], W["mlp2"][:, k, m * P:(m + 1) * P], ones[:, 0:1], start=(k == 0), stop=(k == HT - 1))
            ins.then_inc(S["setup_pe"], 1)
            pe.wait_ge(S["made"], 1)

            def g0(t):
                pe.wait_ge(S["x0Tl"], t + 1)
                wait(pe, S["xnT0"], t)
                product3(bank[0], A0, x0Tp, CT, CT).then_inc(S["g0_mm"], 1)

            def h0_(t):
                pe.wait_ge(S["g0"], t + 1)
                product3(bank[0], x0Tp, WP["W3"], CT, NT).then_inc(S["h0_mm"], 1)

            def s0(t):
                pe.wait_ge(S["h0"], t + 1)
                for m in range(NT):
                    nc.tensor.matmul(bank[0][:, m, :], ident16[:, :], mask16[:, m, :], start=True, stop=False)
                    for k in range(CT):
                        for i, (a, b) in enumerate(((0, 1), (1, 0), (0, 0))):
                            ins = nc.tensor.matmul(bank[0][:, m, :], gT[a][:, k, m * P:(m + 1) * P], x0Tp[b][:, k, :],
                                                   start=False, stop=(k == CT - 1 and i == 2))
                ins.then_inc(S["s0_mm"], 1)

            def t0(t):
                pe.wait_ge(S["pro0"], t + 1)
                transposes(bank[0], pro[0]).then_inc(S["proT0_mm"], 1)

            def a0(t):
                pe.wait_ge(S["proT0"], t + 1)
                product(bank[0], proT[0], h0, NT, NT).then_inc(S["av0_mm"], 1)

            def x0_(t):
                pe.wait_ge(S["xn0"], t + 1)
                transposes(bank[0], xn[0]).then_inc(S["xnT0_mm"], 1)

            def h1_(t):
                pe.wait_ge(S["xnT0"], t + 1)
                wait(pe, S["xnT1"], t)
                product(bank[1], xnT[0], W["W_"], CT, NT).then_inc(S["h1_mm"], 1)

            def f1_(t):
                pe.wait_ge(S["h1"], t + 1)
                columns(bank[1], xnT[0], v1, CT).then_inc(S["f1_mm"], 1)

            def u1_(t):
                pe.wait_ge(S["f1"], t + 1)
                column_row(bank[1][:, 0, 0:P], f1[:, 0, 1:2])
                column_row(bank[1][:, 0, P:2 * P], f1[:, 1, 1:2]).then_inc(S["u1_mm"], 1)

            def t1(t):
                pe.wait_ge(S["pro1"], t + 1)
                transposes(bank[1], pro[1]).then_inc(S["proT1_mm"], 1)

            def a1(t):
                pe.wait_ge(S["proT1"], t + 1)
                product(bank[1], proT[1], h1, NT, NT).then_inc(S["av1_mm"], 1)

            def x1_(t):
                pe.wait_ge(S["xn1"], t + 1)
                transposes(bank[1], xn[1]).then_inc(S["xnT1_mm"], 1)

            def m2(t):
                pe.wait_ge(S["xnT1"], t + 1)
                wait(pe, S["att_b"], t)
                product3(bank[2], WP["mlp1"], xnT[1], CT, 2)
                product3(bank[3], WP["mlp1"], xnT[1], CT, 2, off=2).then_inc(S["o1_mm"], 1)

            def f2(t):
                pe.wait_ge(S["o1T"], t + 1)
                columns(bank[2], o1T, vfc, HT).then_inc(S["ffc_mm"], 1)

            def b2(t):
                pe.wait_ge(S["ffc"], t + 1)
                for c in range(2):
                    for m in range(NT):
                        ins = column_row(bank[2][:, c, m * P:(m + 1) * P], ffc[:, m, c:c + 1])
                ins.then_inc(S["b2_mm"], 1)

            def hidden(m, dst):
                for k in range(HT):
                    for i, (a, b) in enumerate(((0, 1), (1, 0), (0, 0))):
                        ins = nc.tensor.matmul(dst[:, :, :], o1Tp[a][:, k, m * P:(m + 1) * P], WP["fc"][b][:, k, :],
                                               start=(k == 0 and i == 0), stop=(k == HT - 1 and i == 2))
                return ins

            def c2(t):
                pe.wait_ge(S["o1Tl"], t + 1)
                hidden(0, bank[3]).then_inc(S["hfc0_mm"], 1)

            def r2(t):
                pe.wait_ge(S["hfc0"], t + 1)
                hidden(1, bank[3]).then_inc(S["hfc1_mm"], 1)

            def d2(t):
                pe.wait_ge(S["pfcT"], t + 1)
                for k in range(NT):
                    ins = nc.tensor.matmul(bank[2][:, 0, :], ones[:, :], pfcT[:, k, :], start=(k == 0), stop=(k == NT - 1))
                ins.then_inc(S["den2_mm"], 1)

            def v2(t):
                pe.wait_ge(S["hfc1"], t + 1)
                product(bank[3], hfc, pfcT, NT, 2).then_inc(S["av2a_mm"], 1)
                pe.wait_ge(S["rdb"], t + 1)
                product(bank[2], hfc, pfcT, NT, 2, off=2).then_inc(S["av2b_mm"], 1)

            def m3(t):
                pe.wait_ge(S["o2T"], t + 1)
                wait(pe, S["xnT2"], t)
                product3(bank[4], WP["mlp2"], o2T, HT, CT).then_inc(S["o3_mm"], 1)

            def h3_(t):
                pe.wait_ge(S["o3T"], t + 1)
                wait(pe, S["e3"], t)
                product(bank[5], o3T, W["hand"], CT, NT).then_inc(S["h3_mm"], 1)

            def f3_(t):
                columns(bank[4], o3T, vha, CT).then_inc(S["f3_mm"], 1)

            def u3_(t):
                pe.wait_ge(S["f3"], t + 1)
                column_row(bank[4][:, 0, 0:P], f3[:, 0, 1:2])
                column_row(bank[4][:, 0, P:2 * P], f3[:, 1, 1:2]).then_inc(S["u3_mm"], 1)

            def t3(t):
                pe.wait_ge(S["pro2"], t + 1)
                transposes(bank[4], pro[2]).then_inc(S["proT2_mm"], 1)

            def a3(t):
                pe.wait_ge(S["h3"], t + 1)
                transposes(bank[5], o3T).then_inc(S["o3n_mm"], 1)
                pe.wait_ge(S["proT2"], t + 1)
                product(bank[4], proT[2], h3, NT, NT).then_inc(S["av3_mm"], 1)

            def x3_(t):
                pe.wait_ge(S["xn2"], t + 1)
                transposes(bank[4], xn[2]).then_inc(S["xnT2_mm"], 1)

            def q4(t):
                pe.wait_ge(S["xnT2"], t + 1)
                wait(pe, S["y3"], t)
                product3(bank[6], WP["wqT"], xnT[2], CT, CT).then_inc(S["q4_mm"], 1)

            def k4(t):
                wait(pe, S["o4T"], t)
                product3(bank[7], WP["wkT"], xnT[2], CT, CT).then_inc(S["k4_mm"], 1)

            def v4_(t):
                pe.wait_ge(S["qT"], t + 1)
                product3(bank[6], xnT[2], WP["wvT"], CT, NT).then_inc(S["v4_mm"], 1)

            def scores(h):
                b = bank[7 - h % 2]
                rows_ = slice((h % 2) * HD, (h % 2) * HD + HD)
                for m in range(NT):
                    nc.tensor.matmul(b[:, m, :], ident16[:, :], mask3[:, m, :], start=True, stop=False)
                    ins = nc.tensor.matmul(b[:, m, :], qT[rows_, h // 2, m * P:(m + 1) * P], kT[rows_, h // 2, :], start=False, stop=True)
                ins.then_inc(S["sc4_mm"], 1)

            def s40(t):
                pe.wait_ge(S["kT"], t + 1)
                scores(0)

            def s41(t):
                pe.wait_ge(S["v4"], t + 1)
                scores(1)

            def s42(t):
                pe.wait_ge(S["p4T"], HEADS * t + 1)
                scores(2)

            def s43(t):
                pe.wait_ge(S["p4T"], HEADS * t + 2)
                scores(3)

            def t4(h):
                def step(t):
                    pe.wait_ge(S["p4"], HEADS * t + h + 1)
                    transposes(bank[7 - h % 2], p4[:, h, :, :]).then_inc(S["p4T_mm"], 1)
                return step

            def a4(t):
                pe.wait_ge(S["p4T"], HEADS * t + HEADS)
                for h in range(HEADS):
                    for m in range(NT):
                        for k in range(NT):
                            ins = nc.tensor.matmul(bank[6][:, m, h * HD:(h + 1) * HD], p4T[:, h, k, m * P:(m + 1) * P],
                                                   v4[:, k, h * HD:(h + 1) * HD], start=(k == 0), stop=(k == NT - 1))
                ins.then_inc(S["av4_mm"], 1)

            def o4_(t):
                pe.wait_ge(S["o4"], t + 1)
                transposes(bank[7], o4).then_inc(S["o4T_mm"], 1)

            def y4(t):
                pe.wait_ge(S["o4T"], t + 1)
                product(bank[6], o4T, W["woT"], CT, NT).then_inc(S["y4_mm"], 1)

            run(pe, {"g0": g0, "h0": h0_, "s0": s0, "t0": t0, "a0": a0, "x0": x0_,
                     "h1": h1_, "f1": f1_, "u1": u1_, "t1": t1, "a1": a1, "x1": x1_,
                     "m2": m2, "f2": f2, "b2": b2, "c2": c2, "r2": r2, "d2": d2, "v2": v2,
                     "m3": m3, "h3": h3_, "f3": f3_, "u3": u3_, "t3": t3, "a3": a3, "x3": x3_,
                     "q4": q4, "k4": k4, "v4": v4_, "s40": s40, "s41": s41, "s42": s42, "s43": s43,
                     "t40": t4(0), "t41": t4(1), "t42": t4(2), "t43": t4(3), "a4": a4, "o4": o4_, "y4": y4})

        @block.scalar
        def _(ac):
            def copy(dst, src):
                return nc.scalar.activation(dst, src, ACT.Copy)

            def exps(i):
                for m in range(NT):
                    ins = nc.scalar.activation(pro[i][:, m, :], sco[i][:, m, :], ACT.Exp, bias=nmax[i][:, m:m + 1], accum_out=den[i][:, m:m + 1])
                return ins

            ac.wait_ge(S["made"], 1)

            def g0(t):
                ac.wait_ge(S["g0_mm"], t + 1)
                copy(gT[0][:, :, :], bank[0][:, :, :]).then_inc(S["g0h"], 1)

            def l2(t):
                ac.wait_ge(S["x0T_in"], 16 * (t + 1))
                wait(ac, S["s0_mm"], t)
                copy(x0Tp[0][:, :, :], x0T[:, :, :]).then_inc(S["x0Th"], 1)

            def s0(t):
                ac.wait_ge(S["s0_mm"], t + 1)
                copy(raw[0][:, :, :], bank[0][:, :, :]).then_inc(S["raw0"], 1)

            def p0(t):
                ac.wait_ge(S["nmax0"], t + 1)
                exps(0).then_inc(S["pro0"], 1)

            def t0(t):
                ac.wait_ge(S["proT0_mm"], t + 1)
                copy(proT[0][:, :, :], bank[0][:, :, :]).then_inc(S["proT0"], 1)

            def a0(t):
                ac.wait_ge(S["av0_mm"], t + 1)
                ac.wait_ge(S["rden0"], t + 1)
                for m in range(NT):
                    ins = nc.scalar.activation(act[0][:, m, :], bank[0][:, m, :], ACT.Relu, scale=rden[0][:, m:m + 1])
                ins.then_inc(S["act0"], 1)

            def x0_(t):
                ac.wait_ge(S["xnT0_mm"], t + 1)
                copy(xnT[0][:, :, :], bank[0][:, :, :]).then_inc(S["xnT0"], 1)

            def u1_(t):
                ac.wait_ge(S["u1_mm"], t + 1)
                for m in range(NT):
                    ins = nc.scalar.activation(u1[:, m, :], bank[1][:, 0, :], ACT.Identity, bias=f1[:, m, 0:1])
                ins.then_inc(S["u1"], 1)

            def p1(t):
                ac.wait_ge(S["nmax1"], t + 1)
                exps(1).then_inc(S["pro1"], 1)

            def t1(t):
                ac.wait_ge(S["proT1_mm"], t + 1)
                copy(proT[1][:, :, :], bank[1][:, :, :]).then_inc(S["proT1"], 1)

            def a1(t):
                ac.wait_ge(S["av1_mm"], t + 1)
                ac.wait_ge(S["rden1"], t + 1)
                for m in range(NT):
                    ins = nc.scalar.activation(act[1][:, m, :], bank[1][:, m, :], ACT.Exp, scale=rden[1][:, m:m + 1])
                ins.then_inc(S["act1"], 1)

            def x1_(t):
                ac.wait_ge(S["xnT1_mm"], t + 1)
                copy(xnT[1][0][:, :, :], bank[1][:, :, :]).then_inc(S["xnT1h"], 1)

            def m2(t):
                ac.wait_ge(S["o1_mm"], t + 1)
                for m in range(HT):
                    ins = nc.scalar.activation(o1T[:, m, :], bank[2 + m // 2][:, m % 2, :], ACT.Relu, bias=W["b1"][:, m, 0:1])
                ins.then_inc(S["o1T"], 1)
                ac.wait_ge(S["o1T"], t + 1)
                copy(o1Tp[0][:, :, :], o1T[:, :, :]).then_inc(S["o1Th"], 1)

            def c2(t):
                ac.wait_ge(S["hfc0_mm"], t + 1)
                copy(hfc[:, 0, :].rearrange("p (a b) -> p a b", a=2), bank[3][:, :, :]).then_inc(S["hfc0"], 1)

            def r2(t):
                ac.wait_ge(S["np"], t + 1)
                nc.scalar.activation(rows[:, 0, :], neg_pos[:, 0, :], ACT.Exp, scale=1.0 - SLOPE)
                nc.scalar.activation(rows[:, 1, :], neg_pos[:, 1, :], ACT.Exp, scale=-(1.0 - SLOPE)).then_inc(S["rows"], 1)
                ac.wait_ge(S["gap"], t + 1)
                nc.scalar.activation(cols[:, 0, :], gap[:, :], ACT.Exp)
                nc.scalar.activation(cols[:, 1, :], gap[:, :], ACT.Exp, scale=SLOPE).then_inc(S["cols"], 1)
                ac.wait_ge(S["hfc1_mm"], t + 1)
                copy(hfc[:, 1, :].rearrange("p (a b) -> p a b", a=2), bank[3][:, :, :]).then_inc(S["hfc1"], 1)

            def y2(t):
                ac.wait_ge(S["cut"], t + 1)
                nc.scalar.activation(ex1[:, :, :], cut[:, :, :], ACT.Exp).then_inc(S["ex1"], 1)
                ac.wait_ge(S["ex1"], t + 1)
                nc.scalar.activation(ex2[:, :, :], ex1[:, :, :], ACT.Exp, bias=W["m1"][:, 0, 0:1]).then_inc(S["ex2"], 1)

            def z2(t):
                ac.wait_ge(S["o2"], t + 1)
                wait(ac, S["o3_mm"], t)
                copy(o2T[0][:, :, :], o2[:, :, :]).then_inc(S["o2Th"], 1)

            def m3(t):
                ac.wait_ge(S["o3_mm"], t + 1)
                for m in range(CT):
                    ins = nc.scalar.activation(o3T[:, m, :], bank[4][:, m, :], ACT.Relu, bias=b2m[:, m:m + 1])
                ins.then_inc(S["o3T"], 1)

            def u3_(t):
                ac.wait_ge(S["u3_mm"], t + 1)
                for m in range(NT):
                    ins = nc.scalar.activation(u3[:, m, :], bank[4][:, 0, :], ACT.Identity, bias=f3[:, m, 0:1])
                ins.then_inc(S["u3"], 1)

            def p3(t):
                ac.wait_ge(S["nmax2"], t + 1)
                exps(2).then_inc(S["pro2"], 1)

            def t3(t):
                ac.wait_ge(S["proT2_mm"], t + 1)
                copy(proT[2][:, :, :], bank[4][:, :, :]).then_inc(S["proT2"], 1)

            def a3(t):
                ac.wait_ge(S["cut3"], t + 1)
                nc.scalar.activation(act[2][:, :, :], cut3[:, :, :], ACT.Exp).then_inc(S["act2"], 1)
                ac.wait_ge(S["act2"], t + 1)
                nc.scalar.activation(act[2][:, :, :], act[2][:, :, :], ACT.Exp, bias=W["m1"][:, 0, 0:1]).then_inc(S["ex3"], 1)

            def x3_(t):
                ac.wait_ge(S["xnT2_mm"], t + 1)
                copy(xnT[2][0][:, :, :], bank[4][:, :, :]).then_inc(S["xnT2h"], 1)

            def q4(t):
                ac.wait_ge(S["q4_mm"], t + 1)
                for m in range(CT):
                    ins = nc.scalar.activation(qT[:, m, :], bank[6][:, m, :], ACT.Identity, bias=bq8[:, m:m + 1], scale=QSCALE)
                ins.then_inc(S["qT"], 1)

            def k4(t):
                ac.wait_ge(S["k4_mm"], t + 1)
                for m in range(CT):
                    ins = nc.scalar.activation(kT[:, m, :], bank[7][:, m, :], ACT.Identity, bias=W["bk"][:, m, 0:1])
                ins.then_inc(S["kT"], 1)

            def p4_(h):
                def step(t):
                    ac.wait_ge(S["nmx4"], HEADS * t + h + 1)
                    for m in range(NT):
                        ins = nc.scalar.activation(p4[:, h, m, :], bank[7 - h % 2][:, m, :], ACT.Exp,
                                                   bias=nmx4[:, h, m:m + 1], accum_out=den4[:, m, h:h + 1])
                    ins.then_inc(S["p4"], 1)
                return step

            def t4(h):
                def step(t):
                    ac.wait_ge(S["p4T_mm"], HEADS * t + h + 1)
                    copy(p4T[:, h, :, :], bank[7 - h % 2][:, :, :]).then_inc(S["p4T"], 1)
                return step

            def o4_(t):
                ac.wait_ge(S["o4T_mm"], t + 1)
                copy(o4T[:, :, :], bank[7][:, :, :]).then_inc(S["o4T"], 1)

            run(ac, {"l2": l2, "g0": g0, "s0": s0, "p0": p0, "t0": t0, "a0": a0, "x0": x0_,
                     "u1": u1_, "p1": p1, "t1": t1, "a1": a1, "x1": x1_,
                     "m2": m2, "c2": c2, "r2": r2, "y2": y2, "z2": z2,
                     "m3": m3, "u3": u3_, "p3": p3, "t3": t3, "a3": a3, "x3": x3_,
                     "q4": q4, "k4": k4, "p40": p4_(0), "p41": p4_(1), "p42": p4_(2), "p43": p4_(3),
                     "t40": t4(0), "t41": t4(1), "t42": t4(2), "t43": t4(3), "o4": o4_})

        @block.vector
        def _(dv):
            V = nc.vector

            def low_part(pair, whole):
                return V.tensor_tensor(pair[1][:, :, :], whole, pair[0][:, :, :].bitcast(fp32), ALU.subtract)

            dv.wait_ge(S["loaded"], 16 * n_loads)
            V.tensor_copy(ident16[:, :], ident[:, :])
            V.tensor_scalar(mask[:, :, :], adj_sb[:, :, :], 0.0, MASK, ALU.is_le, ALU.mult)
            V.tensor_scalar(mask16[:, :, :], adj_sb[:, :, :], 0.0, MASK, ALU.is_le, ALU.mult)
            V.tensor_scalar(mask3[:, :, :], adj_sb[:, :, :], 0.0, MASK, ALU.is_equal, ALU.mult).then_inc(S["setup_dve"], 1)
            dv.wait_ge(S["setup_dve"], 1)
            V.reduce_max(some3[:, :], mask3[:, :, :], AX.X).then_inc(S["setup_dve"], 1)
            dv.wait_ge(S["setup_dve"], 2)
            V.tensor_scalar(some3[:, :], some3[:, :], 0.0, None, ALU.is_equal)
            V.tensor_scalar(bq8[:, :], W["bq"][:, :, 0], QSCALE, None, ALU.mult)
            dv.wait_ge(S["setup_pe"], 1)
            V.tensor_copy(A0f[:, :, :], bank[0][:, :, :]).then_inc(S["setup_dve"], 1)
            dv.wait_ge(S["setup_dve"], 3)
            full = {**{n: W[n] for n in SPLIT}, "A0": A0f[:, :, :]}
            both = {**WP, "A0": A0}
            for n in full:
                ins = V.tensor_copy(both[n][0][:, :, :], full[n])
            ins.then_inc(S["wsplit"], 1)
            dv.wait_ge(S["wsplit"], 1)
            for n in full:
                low_part(both[n], full[n])
            V.tensor_copy(v1[:, :, :], bank[1][:, :, 0:2])
            V.tensor_copy(vha[:, :, :], bank[2][:, :, 0:2])
            V.tensor_copy(vfc[:, :, :], bank[3][:, 0, 0:2 * HT].rearrange("p (m c) -> p m c", c=2))
            V.tensor_tensor(b2m[:, :], W["b2"][:, :, 0], bank[4][:, 0, 0:CT], ALU.subtract).then_inc(S["made"], 1)

            def leaky(i, s, a, b, t):
                V.scalar_tensor_tensor(sco[i][:, :, :], a, SLOPE, b, ALU.mult, ALU.max).then_inc(s[0], 1)
                dv.wait_ge(s[0], t + 1)
                V.tensor_reduce(nmax[i][:, :], sco[i][:, :, :], AX.X, ALU.max, negate=True).then_inc(s[1], 1)

            def stats(i, s_y, s_st, s_mv, t):
                dv.wait_ge(s_y, t + 1)
                for m in range(NT):
                    ins = V.bn_stats(stat[i][:, m, :], y[i][:, m, :])
                ins.then_inc(s_st, 1)
                dv.wait_ge(S["loaded"], 16)
                dv.wait_ge(s_st, t + 1)
                for m in range(NT):
                    ins = V.bn_aggr(mv[i][:, m, :], stat[i][:, m, :])
                ins.then_inc(s_mv, 1)

            def norm(i):
                for m in range(NT):
                    ins = V.tensor_scalar(xn[i][:, m, :], y[i][:, m, :], mv[i][:, m, 0:1], rstd[i][:, m:m + 1], ALU.subtract, ALU.mult)
                return ins

            def g0(t):
                dv.wait_ge(S["g0h"], t + 1)
                low_part(gT, bank[0][:, :, :]).then_inc(S["g0"], 1)

            def x1_(t):
                dv.wait_ge(S["xnT1h"], t + 1)
                low_part(xnT[1], bank[1][:, :, :]).then_inc(S["xnT1"], 1)

            def x3_(t):
                dv.wait_ge(S["xnT2h"], t + 1)
                low_part(xnT[2], bank[4][:, :, :]).then_inc(S["xnT2"], 1)

            def z2(t):
                dv.wait_ge(S["o2Th"], t + 1)
                low_part(o2T, o2[:, :, :]).then_inc(S["o2T"], 1)

            def h0_(t):
                dv.wait_ge(S["h0_mm"], t + 1)
                V.tensor_copy(h0[:, :, :], bank[0][:, :, :]).then_inc(S["h0"], 1)

            def s0(t):
                dv.wait_ge(S["raw0"], t + 1)
                leaky(0, (S["sco0"], S["nmax0"]), bank[0][:, :, :], raw[0][:, :, :], t)

            def t0(t):
                dv.wait_ge(S["pro0"], t + 1)
                V.reciprocal(rden[0][:, :], den[0][:, :]).then_inc(S["rden0"], 1)

            def a0(t):
                stats(0, S["y0"], S["st0"], S["mv0"], t)

            def n0(t):
                dv.wait_ge(S["rstd0"], t + 1)
                wait(dv, S["y1"], t)
                norm(0).then_inc(S["xn0"], 1)

            def h1_(t):
                dv.wait_ge(S["h1_mm"], t + 1)
                V.tensor_copy(h1[:, :, :], bank[1][:, :, :]).then_inc(S["h1"], 1)

            def f1_(t):
                dv.wait_ge(S["f1_mm"], t + 1)
                V.tensor_copy(f1[:, :, :], bank[1][:, :, 0:2]).then_inc(S["f1"], 1)

            def e1_(t):
                dv.wait_ge(S["raw1"], t + 1)
                leaky(1, (S["sco1"], S["nmax1"]), raw[1][:, :, :], raw[1][:, :, :], t)

            def t1(t):
                dv.wait_ge(S["pro1"], t + 1)
                V.reciprocal(rden[1][:, :], den[1][:, :]).then_inc(S["rden1"], 1)

            def a1(t):
                dv.wait_ge(S["act1"], t + 1)
                for m in range(NT):
                    ins = V.tensor_scalar(q1[:, m, :], bank[1][:, m, :], rden[1][:, m:m + 1], 0.0, ALU.mult, ALU.max)
                ins.then_inc(S["q1"], 1)
                dv.wait_ge(S["q1"], t + 1)
                V.scalar_tensor_tensor(e1[:, :, :], act[1][:, :, :], 1.0, q1[:, :, :], ALU.min, ALU.add).then_inc(S["e1"], 1)
                stats(1, S["y1"], S["st1"], S["mv1"], t)

            def n1(t):
                dv.wait_ge(S["rstd1"], t + 1)
                wait(dv, S["x2b"], t)
                norm(1).then_inc(S["xn1"], 1)

            def f2(t):
                dv.wait_ge(S["ffc_mm"], t + 1)
                V.tensor_copy(ffc[:, :, :], bank[2][:, :, 0:2]).then_inc(S["ffc"], 1)

            def b2(t):
                dv.wait_ge(S["b2_mm"], t + 1)
                V.reduce_max(fmax[:, :], bank[2][:, 1, :], AX.X).then_inc(S["fmax"], 1)
                dv.wait_ge(S["fmax"], t + 1)
                V.tensor_scalar(neg_pos[:, 0, :], bank[2][:, 0, :], fmax[:, 0:1], 0.0, ALU.add, ALU.min)
                V.tensor_scalar(neg_pos[:, 1, :], bank[2][:, 0, :], fmax[:, 0:1], 0.0, ALU.add, ALU.max).then_inc(S["np"], 1)
                V.tensor_scalar(gap[:, :], ffc[:, :, 1], fmax[:, 0:1], None, ALU.subtract).then_inc(S["gap"], 1)

            def w2(t):
                dv.wait_ge(S["rows"], t + 1)
                dv.wait_ge(S["cols"], t + 1)
                for m in range(NT):
                    ins = V.tensor_scalar(low[:, m, :], rows[:, 1, :], cols[:, 1, m:m + 1], None, ALU.mult)
                ins.then_inc(S["low"], 1)
                dv.wait_ge(S["low"], t + 1)
                for m in range(NT):
                    ins = V.scalar_tensor_tensor(pfcT[:, m, :], rows[:, 0, :], cols[:, 0, m:m + 1], low[:, m, :], ALU.mult, ALU.max)
                ins.then_inc(S["pfcT"], 1)

            def v2(t):
                dv.wait_ge(S["den2_mm"], t + 1)
                V.reciprocal(rdb[:, :], bank[2][:, 0, :]).then_inc(S["rdb"], 1)
                dv.wait_ge(S["rdb"], t + 1)
                rb = rdb[:, :].unsqueeze(1).broadcast_to([P, 2, N])
                dv.wait_ge(S["av2a_mm"], t + 1)
                V.tensor_tensor(att[:, 0:2, :], bank[3][:, :, :], rb, ALU.mult).then_inc(S["att_a"], 1)
                dv.wait_ge(S["av2b_mm"], t + 1)
                V.tensor_tensor(att[:, 2:4, :], bank[2][:, :, :], rb, ALU.mult).then_inc(S["att_b"], 1)

            def i2(t):
                dv.wait_ge(S["att_b"], t + 1)
                V.tensor_scalar(cut[:, :, :], att[:, :, :], 0.0, None, ALU.min).then_inc(S["cut"], 1)
                V.scalar_tensor_tensor(res[:, :, :], att[:, :, :], 0.0, o1T[:, :, :], ALU.max, ALU.add).then_inc(S["res"], 1)

            def h3_(t):
                dv.wait_ge(S["h3_mm"], t + 1)
                V.tensor_copy(h3[:, :, :], bank[5][:, :, :]).then_inc(S["h3"], 1)

            def f3_(t):
                dv.wait_ge(S["f3_mm"], t + 1)
                V.tensor_copy(f3[:, :, :], bank[4][:, :, 0:2]).then_inc(S["f3"], 1)

            def e3_(t):
                dv.wait_ge(S["raw2"], t + 1)
                leaky(2, (S["sco2"], S["nmax2"]), raw[2][:, :, :], raw[2][:, :, :], t)

            def t3(t):
                dv.wait_ge(S["pro2"], t + 1)
                V.reciprocal(rden[2][:, :], den[2][:, :]).then_inc(S["rden2"], 1)

            def a3(t):
                dv.wait_ge(S["rden2"], t + 1)
                dv.wait_ge(S["av3_mm"], t + 1)
                for m in range(NT):
                    ins = V.tensor_scalar(cut3[:, m, :], bank[4][:, m, :], rden[2][:, m:m + 1], 0.0, ALU.mult, ALU.min)
                ins.then_inc(S["cut3"], 1)
                for m in range(NT):
                    ins = V.tensor_scalar(q3[:, m, :], bank[4][:, m, :], rden[2][:, m:m + 1], 0.0, ALU.mult, ALU.max)
                ins.then_inc(S["q3"], 1)
                dv.wait_ge(S["q3"], t + 1)
                dv.wait_ge(S["o3n_mm"], t + 1)
                V.scalar_tensor_tensor(r3[:, :, :], q3[:, :, :], -1.0, bank[5][:, :, :], ALU.add, ALU.add).then_inc(S["r3"], 1)

            def z3(t):
                dv.wait_ge(S["e3"], t + 1)
                dv.wait_ge(S["x2b"], t + 1)
                V.scalar_tensor_tensor(y[2][:, :, :], e3[:, :, :], 0.0, x2b[:, :, :], ALU.max, ALU.add).then_inc(S["y2"], 1)
                stats(2, S["y2"], S["st2"], S["mv2"], t)

            def n3(t):
                dv.wait_ge(S["rstd2"], t + 1)
                wait(dv, S["xb4"], t)
                norm(2).then_inc(S["xn2"], 1)

            def v4_(t):
                dv.wait_ge(S["v4_mm"], t + 1)
                V.tensor_tensor(v4[:, :, :], bank[6][:, :, :], W["bv"][:, 0:1, :].broadcast_to([P, NT, C]), ALU.add).then_inc(S["v4"], 1)

            def s4(h):
                def step(t):
                    dv.wait_ge(S["sc4_mm"], HEADS * t + h + 1)
                    V.tensor_reduce(nmx4[:, h, :], bank[7 - h % 2][:, :, :], AX.X, ALU.max, negate=True).then_inc(S["nmx4"], 1)
                return step

            def a4(t):
                dv.wait_ge(S["p4"], HEADS * t + HEADS)
                V.reciprocal(den4[:, :, :], den4[:, :, :]).then_inc(S["rd4a"], 1)
                dv.wait_ge(S["rd4a"], t + 1)
                V.tensor_tensor(rd4[:, :, :], den4[:, :, :], some3[:, :].unsqueeze(2).broadcast_to([P, NT, HEADS]), ALU.mult).then_inc(S["rd4"], 1)
                dv.wait_ge(S["rd4"], t + 1)
                dv.wait_ge(S["av4_mm"], t + 1)
                V.tensor_tensor(o4[:, :, :].rearrange("p t (h d) -> p (t h) d", h=HEADS),
                                bank[6][:, :, :].rearrange("p t (h d) -> p (t h) d", h=HEADS),
                                rd4[:, :, :].rearrange("p t h -> p (t h)").unsqueeze(2).broadcast_to([P, NT * HEADS, HD]),
                                ALU.mult).then_inc(S["o4"], 1)

            def y4(t):
                dv.wait_ge(S["y4_mm"], t + 1)
                dv.wait_ge(S["xb4"], t + 1)
                V.tensor_tensor(y[3][:, :, :], bank[6][:, :, :], xb4[:, :, :], ALU.add).then_inc(S["y3"], 1)
                stats(3, S["y3"], S["st3"], S["mv3"], t)

            def n4(t):
                dv.wait_ge(S["rstd3"], t + 1)
                wait(dv, S["stored"], 16 * t)
                norm(3).then_inc(S["xn3"], 1)

            run(dv, {"g0": g0, "x1": x1_, "x3": x3_, "z2": z2, "h0": h0_, "s0": s0, "t0": t0, "a0": a0, "n0": n0,
                     "h1": h1_, "f1": f1_, "e1": e1_, "t1": t1, "a1": a1, "n1": n1,
                     "f2": f2, "b2": b2, "w2": w2, "v2": v2, "i2": i2,
                     "h3": h3_, "f3": f3_, "e3": e3_, "t3": t3, "a3": a3, "z3": z3, "n3": n3,
                     "v4": v4_, "s40": s4(0), "s41": s4(1), "s42": s4(2), "s43": s4(3), "a4": a4, "y4": y4, "n4": n4})

        @block.gpsimd
        def _(po):
            G = nc.gpsimd
            G.memset(eps[:, :], EPS)
            G.memset(mhalf[:, :], -0.5)
            G.memset(zeros[:, :, :], 0.0)
            G.memset(ones[:, :], 1.0).then_inc(S["setup_pool"], 1)
            po.wait_ge(S["setup_pool"], 1)
            po.wait_ge(S["made"], 1)

            def inv_std(i, s_mv, s_ve, s_rs, t):
                po.wait_ge(s_mv, t + 1)
                G.tensor_tensor(vare[i][:, :], mv[i][:, :, 1], eps[:, :], ALU.add).then_inc(s_ve, 1)
                po.wait_ge(s_ve, t + 1)
                G.tensor_tensor(rstd[i][:, :], vare[i][:, :], mhalf[:, :], ALU.pow).then_inc(s_rs, 1)

            def a0(t):
                po.wait_ge(S["x0_in"], 16 * (t + 1))
                po.wait_ge(S["act0"], t + 1)
                G.tensor_tensor(y[0][:, :, :], act[0][:, :, :], x0[:, :, :], ALU.add).then_inc(S["y0"], 1)
                inv_std(0, S["mv0"], S["vare0"], S["rstd0"], t)

            def u1_(t):
                po.wait_ge(S["u1"], t + 1)
                G.tensor_tensor(raw[1][:, :, :], u1[:, :, :], mask[:, :, :], ALU.add).then_inc(S["raw1"], 1)

            def a1(t):
                po.wait_ge(S["e1"], t + 1)
                G.tensor_tensor(y[1][:, :, :], e1[:, :, :], xn[0][:, :, :], ALU.add).then_inc(S["y1"], 1)
                inv_std(1, S["mv1"], S["vare1"], S["rstd1"], t)

            def i2(t):
                wait(po, S["y2"], t)
                po.wait_ge(S["xn1"], t + 1)
                G.tensor_tensor(x2b[:, :, :], xn[1][:, :, :], zeros[:, :, :].broadcast_to([P, NT, C]), ALU.add).then_inc(S["x2b"], 1)

            def z2(t):
                po.wait_ge(S["ex2"], t + 1)
                po.wait_ge(S["res"], t + 1)
                wait(po, S["o2T"], t)
                G.tensor_tensor(o2[:, :, :], ex2[:, :, :], res[:, :, :], ALU.add).then_inc(S["o2"], 1)

            def m2(t):
                po.wait_ge(S["o1Th"], t + 1)
                G.tensor_tensor(o1Tp[1][:, :, :], o1T[:, :, :], o1Tp[0][:, :, :].bitcast(fp32), ALU.subtract).then_inc(S["o1Tl"], 1)

            def l2(t):
                po.wait_ge(S["x0Th"], t + 1)
                G.tensor_tensor(x0Tp[1][:, :, :], x0T[:, :, :], x0Tp[0][:, :, :].bitcast(fp32), ALU.subtract).then_inc(S["x0Tl"], 1)

            def u3_(t):
                po.wait_ge(S["u3"], t + 1)
                G.tensor_tensor(raw[2][:, :, :], u3[:, :, :], mask[:, :, :], ALU.add).then_inc(S["raw2"], 1)

            def a3(t):
                po.wait_ge(S["ex3"], t + 1)
                po.wait_ge(S["r3"], t + 1)
                G.tensor_tensor(e3[:, :, :], act[2][:, :, :], r3[:, :, :], ALU.add).then_inc(S["e3"], 1)

            def z3(t):
                inv_std(2, S["mv2"], S["vare2"], S["rstd2"], t)

            def k4(t):
                po.wait_ge(S["xn2"], t + 1)
                G.tensor_tensor(xb4[:, :, :], xn[2][:, :, :], W["bo"][:, 0:1, :].broadcast_to([P, NT, C]), ALU.add).then_inc(S["xb4"], 1)

            def y4(t):
                inv_std(3, S["mv3"], S["vare3"], S["rstd3"], t)

            run(po, {"m2": m2, "l2": l2, "a0": a0, "u1": u1_, "a1": a1, "i2": i2, "z2": z2, "u3": u3_, "a3": a3, "z3": z3, "k4": k4, "y4": y4})


def kernel(**inputs):
    import numpy as np
    import concourse.bacc as bacc
    from concourse.bass_utils import run_bass_kernel_spmd

    a = {n: np.asarray(v) for n, v in inputs.items()}
    x = a["x"]
    column = lambda v: v.reshape(-1, 1)
    spread = lambda v: np.repeat(v.reshape(1, -1), P, axis=0)
    layout = {
        "W1T": a["L0_gnn_W1"].T, "W2T": a["L0_gnn_W2"].T, "W3": a["L0_gnn_W3"],
        "W_": a["L1_gnn_W"], "W_T": a["L1_gnn_W"].T, "a1": a["L1_gnn_a"].reshape(2, -1).T,
        "mlp1": a["L2_gnn_mlp1_w"], "b1": column(a["L2_gnn_mlp1_b"]),
        "fc": a["L2_gnn_W_fc"], "fc_T": a["L2_gnn_W_fc"].T, "afc": a["L2_gnn_a_fc"].reshape(2, -1).T,
        "mlp2": a["L2_gnn_mlp2_w"], "b2": column(a["L2_gnn_mlp2_b"]),
        "hand": a["L2_gnn_W_hand"], "hand_T": a["L2_gnn_W_hand"].T, "ahand": a["L2_gnn_a_hand"].reshape(2, -1).T,
        "wqT": a["L3_gnn_wq"].T, "bq": column(a["L3_gnn_bq"]),
        "wkT": a["L3_gnn_wk"].T, "bk": column(a["L3_gnn_bk"]),
        "wvT": a["L3_gnn_wv"].T, "bv": spread(a["L3_gnn_bv"]),
        "woT": a["L3_gnn_wo"].T, "bo": spread(a["L3_gnn_bo"]),
        "m1": np.full((P, 1), -1.0, np.float32),
    }
    nc = bacc.Bacc("TRN2", target_bir_lowering=False, num_devices=1)
    arrays = {}

    def dram(name, v):
        arrays[name] = np.ascontiguousarray(v)
        return nc.dram_tensor(name, v.shape, mybir.dt.from_np(v.dtype), kind="ExternalInput").ap()

    tiled = lambda v: np.swapaxes(v.reshape(*v.shape[:-2], -1, P, v.shape[-1]), -3, -2)
    weights = {n: dram("in_" + n, tiled(v)) for n, v in layout.items()}
    ins = [dram("in_x", tiled(x)), dram("in_xT", tiled(np.transpose(x, (0, 2, 1)))), dram("in_adj", tiled(a["adj"])),
           dram("in_ident", np.eye(P, dtype=np.float32))]
    out = nc.dram_tensor("out", x.shape, mybir.dt.from_np(x.dtype), kind="ExternalOutput").ap()
    graph_stack(nc, *ins, weights, out)
    return run_bass_kernel_spmd(nc, [arrays], core_ids=[0]).results[0]["out"]
```

```python
import concourse.bass as bass
from concourse import mybir
from contextlib import ExitStack

P = 128


def graph_stack(nc, x, xT, adj, ident_d, weights, out):
    fp32 = mybir.dt.float32
    f32r = mybir.dt.float32r
    bf16 = mybir.dt.bfloat16
    i32 = mybir.dt.int32
    ALU = mybir.AluOpType
    ACT = mybir.ActivationFunctionType
    AX = mybir.AxisListType

    B, N, C = out.shape
    NT = N // P
    CT = C // P
    H2 = weights["mlp1"].shape[2]
    HT = H2 // P
    HEADS = 4
    HD = C // HEADS
    MASK = -(2.0 ** 100)
    SLOPE = 0.2
    EPS = 1e-5
    QSCALE = HD ** -0.5
    STAGES = 6

    with ExitStack() as ctx:
        def sb(name, shape, dt=fp32):
            return ctx.enter_context(nc.sbuf_tensor(name, shape, dt))

        SETUP_ONLY = ("W1T", "W2T", "W_T", "hand_T", "fc_T", "fc", "mlp1", "mlp2", "wqT", "wkT", "wvT", "W3", "W_", "hand", "woT")
        W = {n: sb("w_" + n, list(w.shape)) for n, w in weights.items() if n not in SETUP_ONLY}
        def parts(name, shape):
            return sb(name + "_hi", shape, f32r), sb(name + "_lo", shape, f32r)
        SPLIT = ("fc", "mlp1", "mlp2", "wqT", "wkT", "wvT", "W3", "W_", "hand", "woT")
        WP = {n: parts("w_" + n, list(weights[n].shape)) for n in SPLIT}
        ident = sb("ident", [P, P])
        ident16 = sb("ident16", [P, P], bf16)
        ones = sb("ones", [P, P])
        mask16 = sb("mask16", [P, NT, N], bf16)
        mask3 = sb("mask3", [P, NT, N], bf16)
        some3 = sb("some3", [P, NT])
        eps = sb("eps", [P, NT])
        mhalf = sb("mhalf", [P, NT])
        A0 = parts("A0", [P, CT, C])
        v1 = parts("v1", [P, CT, 2])
        vfc = parts("vfc", [P, HT, 2])
        vha = parts("vha", [P, CT, 2])
        ones2 = sb("ones2", [P, P], f32r)
        b2m = sb("b2m", [P, CT])
        bq8 = sb("bq8", [P, CT])

        x0T = sb("x0T", [P, CT, N])
        x0 = sb("x0", [P, NT, C])
        x0Tp = parts("x0Tp", [P, CT, N])
        gT = parts("gT", [P, CT, N])
        h0 = parts("h0", [P, NT, C])
        o3Tp = parts("o3Tp", [P, CT, N])
        sco = [sb(f"sco{i}", [P, NT, N]) for i in range(3)]
        pro = raw = sco
        proT = [gT, parts("proT1", [P, NT, N]), o3Tp]
        nmax = [sb(f"nmax{i}", [P, NT]) for i in range(3)]
        den = [sb(f"den{i}", [P, NT]) for i in range(3)]
        rden = [sb(f"rden{i}", [P, NT]) for i in range(3)]
        act = [sb(f"act{i}", [P, NT, C]) for i in range(3)]
        A0f = act[1]
        xb4 = sb("xb4", [P, NT, C])
        y = [act[0], sb("y1", [P, NT, C]), sb("y2", [P, NT, C]), xb4]
        stat = [sb(f"stat{i}", [P, NT, 6]) for i in range(4)]
        mv = [sb(f"mv{i}", [P, NT, 2]) for i in range(4)]
        vare = [sb(f"vare{i}", [P, NT]) for i in range(4)]
        rstd = [sb(f"rstd{i}", [P, NT]) for i in range(4)]
        xn = [sb(f"xn{i}", [P, NT, C]) for i in range(3)] + [y[3]]
        xnT = [parts("xnT0", [P, CT, N]), parts("xnT1", [P, CT, N]), parts("xnT2", [P, CT, N])]
        h1 = parts("h1", [P, NT, C])
        src1, dst1 = sco[1][0:2, 0, :], sco[1][0:2, 1, :]
        q1 = e1 = y[1]
        o1T = sb("o1T", [P, HT, N])
        o1Tp = parts("o1Tp", [P, HT, N])
        hfc = parts("hfc", [P, NT, H2])
        fmax_row = sb("fmax_row", [2, 1])
        fmax = sb("fmax", [P, 1])
        neg_pos = sb("neg_pos", [P, 2, N])
        rows = neg_pos
        ffc = neg_pos[0:2, 0, :]
        gap = sb("gap", [P, NT])
        cols = sb("cols", [P, 2, NT])
        low = sb("low", [P, NT, N])
        pfcT = low
        pfcTp = [p[:, 0:NT, :] for p in o1Tp]
        rdb = sb("rdb", [P, N])
        att_cut = sb("att_cut", [P, 2, HT, N])
        att, cut = att_cut[:, 0, :, :], att_cut[:, 1, :, :]
        res, ex1, ex2 = att, cut, cut
        o2 = att
        o2T = parts("o2T", [P, HT, N])
        x2b = sb("x2b", [P, NT, C])
        o3T = sb("o3T", [P, CT, N])
        h3 = parts("h3", [P, NT, C])
        src3, dst3 = sco[2][0:2, 0, :], sco[2][0:2, 1, :]
        q3 = r3 = e3 = y[2]
        cut3 = act[2]
        v4 = sb("v4", [P, NT, C])
        nmx4 = sb("nmx4", [P, HEADS, NT])
        p4 = sb("p4", [P, 2, NT, N])
        p4T = sb("p4T", [P, HEADS, NT, N])
        den4 = sb("den4", [P, HEADS, NT])
        rd4 = sb("rd4", [P, HEADS, NT])
        o4T = parts("o4T", [P, CT, N])
        qT = sb("qT_hi", [P, CT, N], f32r), o4T[0]
        kT = sb("kT_hi", [P, CT, N], f32r), o4T[1]
        W.update({n: p4T[:, i, :, :] for i, n in enumerate(SETUP_ONLY[:HEADS])})
        W.update({"fc": att_cut[:, :, :, :].rearrange("p a (b h) n -> p (a b) (h n)", h=2), "mlp2": p4[:, :, :, :].rearrange("p a b n -> p (a b) n"),
                  "mlp1": o1T[:, :, :].rearrange("p (a b) n -> p a (b n)", a=2), "wqT": sco[0][:, :, :], "wkT": sco[1][:, :, :], "wvT": sco[2][:, :, :],
                  "W3": act[0][:, :, :], "W_": y[1][:, :, :], "hand": y[2][:, :, :], "woT": xn[0][:, :, :]})
        fcT_tiles = [b.rearrange("p t n -> p (t n)") for b in (act[2][:, :, :], o3T[:, :, :], v4[:, :, :], x2b[:, :, :])]
        adj_sb = xn[1][:, :, :].bitcast(i32)

        bank = [ctx.enter_context(nc.psum_tensor(f"bank{i}", [P, 2, 256], fp32)) for i in range(8)]

        names = """loaded made setup_pe setup_dve setup_pool
 x0_in x0T_in x0Th x0Tl g0h xnT1h xnT2h o1Th o1Tl o2 o2Th wsplit xnT0h h0h h1h h3h proT0h proT1h proT2h o3Th o3Tl hfch pfcTf pfcTh o4Th
 g0_mm g0 h0_mm h0 s0_mm raw0 nmax0 pro0 proT0_mm proT0 rden0 av0_mm act0 y0 mv0 rstd0 xn0 xnT0_mm xnT0
 h1_mm h1 f1_mm rows1 u1_mm raw1 nmax1 pro1 proT1_mm proT1 rden1 av1_mm act1 e1 y1 mv1 rstd1 xn1 xnT1_mm xnT1
 o1_mm o1T ffc_mm ffcr fmaxr b2_mm fmax np gap rows cols low pfcT hfc_mm hfc den2_mm rdb
 av2a_mm av2b_mm att_b cut ex1 ex2 res o2T x2b
 o3_mm o3T h3_mm h3 f3_mm rows3 u3_mm raw2 nmax2 pro2 proT2_mm proT2 rden2 av3_mm o3n_mm cut3 act2 ex3 q3 r3 e3 y2 mv2 rstd2 xn2 xnT2_mm xnT2
 q4_mm qTh qT k4_mm kTh kT v4_mm v4 sc4_mm nmx4 p4 p4T_mm p4T rd4a rd4 p4n av4_mm o4T xb4 y4_mm y3 mv3 rstd3 xn3 stored""".split()
        S = {n: ctx.enter_context(nc.semaphore("s_" + n)) for n in names}
        block = ctx.enter_context(nc.Block())

        def wait(eng, sem, n):
            if not (isinstance(n, int) and n <= 0):
                eng.wait_ge(sem, n)

        STEPS = [
            "l0 l2 l1".split(),
            "g0 h0 s0 p0 t0 a0 st0 n0 x0".split(),
            "h1 f1 u1 e1 p1 t1 a1 y1 st1 n1 x1".split(),
            "m2 f2 b2 c2 rc2 r2 w2 d2 j2 v2 vb2 i2 y2 z2".split(),
            "m3 h3 f3 u3 e3 p3 t3 on3 a3 r3 z3 st3 n3 x3".split(),
            "q4 k4 v4 s40 s41 p40 p41 t40 t41 s42 s43 p42 p43 t42 t43 a4 y4 st4 n4".split(),
        ]
        ORDERS = {
            "pe": """
                m2 g0 h1 q4 k4 m3 h0 f1 f2 h3 f3 u1 v4 u3 s0 s40 b2 t3 c2 on3 a3 t40 t41 t1 t0 s42 a1 r2 a0 t42 t43
                a4 x3 d2 v2 y4 x1 vb2 x0
            """,
            "ac": """
                m2 g0 h1 q4 m3 k4 f1 f2 h0 h3 f3 u1 u3 s0 p3 p1 t3 p40 p41 c2 p0 t40 t41 t1 t0 a3 p42 p43 a1 rc2 r2
                l2 a0 t42 t43 w2 j2 a4 x1 x0 y2 x3 z2
            """,
            "dv": """
                g0 h1 f2 q4 h0 h3 k4 v4 e1 e3 s0 s40 s41 t3 p40 p41 b2 c2 a3 r3 t1 t0 s42 s43 z3 p42 st3 p43 a1 r2
                w2 st1 n3 st0 a4 n1 v2 n0 x1 vb2 i2 x0 x3 y4 st4 z2 n4
            """,
            "po": """
                m2 m3 p40 p41 t41 a3 p42 p43 st3 y1 a0 w2 st1 st0 l2 z2 st4
            """,
            "sp": """
                l0 l1 n4
            """,
        }
        STAGE = {name: s for s, steps in enumerate(STEPS) for name in steps}

        def run(eng, order, steps):
            order = order.split()
            assert sorted(order) == sorted(steps)

            def slot(k, active):
                for name in order:
                    if STAGE[name] in active:
                        steps[name](k - STAGE[name])
            first = STAGES
            for k in range(first):
                slot(k, [s for s in range(STAGES) if 0 <= k - s])
            with eng.Fori(first, B) as k:
                slot(k, range(STAGES))
            for k in range(B, B + STAGES - 1):
                slot(k, [s for s in range(STAGES) if k - s < B])

        n_loads = len(weights) - 1 + HT + 2

        @block.sync
        def _(sp):
            for n, w in weights.items():
                if n != "fc_T":
                    sp.dma_start(W[n][:, :, :], w).then_inc(S["loaded"], 16)
            for k in range(HT):
                sp.dma_start(fcT_tiles[k], weights["fc_T"][:, k, :]).then_inc(S["loaded"], 16)
            sp.dma_start(adj_sb, adj).then_inc(S["loaded"], 16)
            sp.dma_start(ident[:, :], ident_d).then_inc(S["loaded"], 16)

            def load_x0T(t):
                wait(sp, S["x0Tl"], t)
                sp.dma_start(x0T[:, :, :], xT[t]).then_inc(S["x0T_in"], 16)

            def load_x0(t):
                wait(sp, S["y0"], t)
                sp.dma_start(x0[:, :, :], x[t]).then_inc(S["x0_in"], 16)

            def store(t):
                wait(sp, S["xn3"], t + 1)
                sp.dma_start(out[t].rearrange("(t p) c -> p t c", p=P), xn[3][:, :, :]).then_inc(S["stored"], 16)

            run(sp, ORDERS["sp"], {"l0": load_x0T, "l1": load_x0, "n4": store})
            sp.wait_ge(S["stored"], 16 * B)

        @block.tensor
        def _(pe):
            def product(dst, lhs, rhs, kt, mt):
                for m in range(mt):
                    for k in range(kt):
                        ins = nc.tensor.matmul(dst[:, m, :], lhs[:, k, m * P:(m + 1) * P], rhs[:, k, :], start=(k == 0), stop=(k == kt - 1))
                return ins

            def product3(dst, lhs, rhs, kt, mt, off=0):
                for m in range(mt):
                    for k in range(kt):
                        for i, (a, b) in enumerate(((0, 1), (1, 0), (0, 0))):
                            ins = nc.tensor.matmul(dst[:, m, :], lhs[a][:, k, (off + m) * P:(off + m + 1) * P], rhs[b][:, k, :],
                                                   start=(k == 0 and i == 0), stop=(k == kt - 1 and i == 2))
                return ins

            def transposes(dst, src):
                for a in range(2):
                    for b in range(2):
                        ins = nc.tensor.transpose(dst[:, b, a * P:(a + 1) * P], src[:, a, b * P:(b + 1) * P], ident[:, :])
                return ins

            def two_rows(dst, vec, xT, kt):
                for k in range(kt):
                    for i, (a, b) in enumerate(((0, 1), (1, 0), (0, 0))):
                        ins = nc.tensor.matmul(dst, vec[a][:, k, :], xT[b][:, k, :], start=(k == 0 and i == 0), stop=(k == kt - 1 and i == 2))
                return ins

            def outer_sum(dst, src_rows, dst_rows):
                nc.tensor.matmul(dst[:, :, :], ident16[:, :], mask16[:, :, :], start=True, stop=False)
                for m in range(NT):
                    ins = nc.tensor.matmul(dst[:, m, :], src_rows[:, m * P:(m + 1) * P], dst_rows[:, :], start=False, stop=(m == NT - 1))
                return ins

            pe.wait_ge(S["loaded"], 16 * n_loads)
            product(bank[0], W["W1T"], W["W2T"], CT, CT)
            for m in range(CT):
                for k in range(CT):
                    nc.tensor.matmul(bank[1][:, m, 0:2], W["W_T"][:, k, m * P:(m + 1) * P], W["a1"][:, k, :], start=(k == 0), stop=(k == CT - 1))
                    nc.tensor.matmul(bank[2][:, m, 0:2], W["hand_T"][:, k, m * P:(m + 1) * P], W["ahand"][:, k, :], start=(k == 0), stop=(k == CT - 1))
            for m in range(HT):
                for k in range(HT):
                    nc.tensor.matmul(bank[3][:, 0, 2 * m:2 * m + 2], fcT_tiles[k][:, m * P:(m + 1) * P], W["afc"][:, k, :], start=(k == 0), stop=(k == HT - 1))
            pe.wait_ge(S["setup_pool"], 1)
            for m in range(CT):
                for k in range(HT):
                    ins = nc.tensor.matmul(bank[4][:, 0, m:m + 1], W["mlp2"][:, k, m * P:(m + 1) * P], ones[:, 0:1], start=(k == 0), stop=(k == HT - 1))
            ins.then_inc(S["setup_pe"], 1)
            pe.wait_ge(S["made"], 1)

            def g0(t):
                pe.wait_ge(S["x0Tl"], t + 1)
                wait(pe, S["xnT0"], t)
                product3(bank[0], A0, x0Tp, CT, CT).then_inc(S["g0_mm"], 1)

            def h0_(t):
                pe.wait_ge(S["g0"], t + 1)
                product3(bank[0], x0Tp, WP["W3"], CT, NT).then_inc(S["h0_mm"], 1)

            def s0(t):
                pe.wait_ge(S["h0"], t + 1)
                nc.tensor.matmul(bank[0][:, :, :], ident16[:, :], mask16[:, :, :], start=True, stop=False)
                for m in range(NT):
                    for k in range(CT):
                        for i, (a, b) in enumerate(((0, 1), (1, 0), (0, 0))):
                            ins = nc.tensor.matmul(bank[0][:, m, :], gT[a][:, k, m * P:(m + 1) * P], x0Tp[b][:, k, :],
                                                   start=False, stop=(m == NT - 1 and k == CT - 1 and i == 2))
                ins.then_inc(S["s0_mm"], 1)

            def t0(t):
                pe.wait_ge(S["pro0"], t + 1)
                transposes(bank[0], pro[0]).then_inc(S["proT0_mm"], 1)

            def a0(t):
                pe.wait_ge(S["proT0"], t + 1)
                product3(bank[0], proT[0], h0, NT, NT).then_inc(S["av0_mm"], 1)

            def x0_(t):
                pe.wait_ge(S["xn0"], t + 1)
                transposes(bank[0], xn[0]).then_inc(S["xnT0_mm"], 1)

            def h1_(t):
                pe.wait_ge(S["xnT0"], t + 1)
                wait(pe, S["xnT1"], t)
                product3(bank[1], xnT[0], WP["W_"], CT, NT).then_inc(S["h1_mm"], 1)

            def f1_(t):
                pe.wait_ge(S["h1"], t + 1)
                two_rows(bank[1][0:2, 0, :], v1, xnT[0], CT).then_inc(S["f1_mm"], 1)

            def u1_(t):
                pe.wait_ge(S["rows1"], t + 1)
                outer_sum(bank[1], src1, dst1).then_inc(S["u1_mm"], 1)

            def t1(t):
                pe.wait_ge(S["pro1"], t + 1)
                transposes(bank[1], pro[1]).then_inc(S["proT1_mm"], 1)

            def a1(t):
                pe.wait_ge(S["proT1"], t + 1)
                product3(bank[1], proT[1], h1, NT, NT).then_inc(S["av1_mm"], 1)

            def x1_(t):
                pe.wait_ge(S["xn1"], t + 1)
                transposes(bank[1], xn[1]).then_inc(S["xnT1_mm"], 1)

            def m2(t):
                pe.wait_ge(S["xnT1"], t + 1)
                wait(pe, S["att_b"], t)
                product3(bank[2], WP["mlp1"], xnT[1], CT, 2)
                product3(bank[3], WP["mlp1"], xnT[1], CT, 2, off=2).then_inc(S["o1_mm"], 1)

            def f2(t):
                pe.wait_ge(S["o1Tl"], t + 1)
                two_rows(bank[2][0:2, 0, :], vfc, o1Tp, HT).then_inc(S["ffc_mm"], 1)

            def b2(t):
                pe.wait_ge(S["fmaxr"], t + 1)
                nc.tensor.matmul(bank[2][:, 0, :], ident[0:2, 0:1].broadcast_to([2, P]), ffc, start=True, stop=True)
                nc.tensor.matmul(bank[2][:, 1, 0:1], ident[0:2, 1:2].broadcast_to([2, P]), fmax_row[:, :], start=True, stop=True)
                for m in range(NT):
                    ins = nc.tensor.transpose(bank[2][:, 1, 2 + 2 * m:4 + 2 * m], ffc[:, m * P:(m + 1) * P], ident[0:2, 0:2])
                ins.then_inc(S["b2_mm"], 1)

            def hidden(m, dst):
                for k in range(HT):
                    for i, (a, b) in enumerate(((0, 1), (1, 0), (0, 0))):
                        ins = nc.tensor.matmul(dst[:, :, :], o1Tp[a][:, k, m * P:(m + 1) * P], WP["fc"][b][:, k, :],
                                               start=(k == 0 and i == 0), stop=(k == HT - 1 and i == 2))
                return ins

            def c2(t):
                hidden(0, bank[3]).then_inc(S["hfc_mm"], 1)

            def r2(t):
                pe.wait_ge(S["hfc"], 2 * t + 1)
                hidden(1, bank[3]).then_inc(S["hfc_mm"], 1)

            def d2(t):
                pe.wait_ge(S["pfcT"], t + 1)
                for k in range(NT):
                    for i in (1, 0):
                        ins = nc.tensor.matmul(bank[2][:, 0, :], ones2[:, :], pfcTp[i][:, k, :], start=(k == 0 and i == 1), stop=(k == NT - 1 and i == 0))
                ins.then_inc(S["den2_mm"], 1)

            def v2(t):
                pe.wait_ge(S["hfc"], 2 * t + 2)
                product3(bank[3], hfc, pfcTp, NT, 2).then_inc(S["av2a_mm"], 1)

            def vb2(t):
                pe.wait_ge(S["rdb"], t + 1)
                product3(bank[2], hfc, pfcTp, NT, 2, off=2).then_inc(S["av2b_mm"], 1)

            def m3(t):
                pe.wait_ge(S["o2T"], t + 1)
                wait(pe, S["xnT2"], t)
                product3(bank[4], WP["mlp2"], o2T, HT, CT).then_inc(S["o3_mm"], 1)

            def h3_(t):
                pe.wait_ge(S["o3Tl"], t + 1)
                wait(pe, S["e3"], t)
                product3(bank[5], o3Tp, WP["hand"], CT, NT).then_inc(S["h3_mm"], 1)

            def f3_(t):
                two_rows(bank[4][0:2, 0, :], vha, o3Tp, CT).then_inc(S["f3_mm"], 1)

            def u3_(t):
                pe.wait_ge(S["rows3"], t + 1)
                outer_sum(bank[4], src3, dst3).then_inc(S["u3_mm"], 1)

            def t3(t):
                pe.wait_ge(S["pro2"], t + 1)
                transposes(bank[4], pro[2]).then_inc(S["proT2_mm"], 1)

            def on3(t):
                pe.wait_ge(S["h3"], t + 1)
                transposes(bank[5], o3T).then_inc(S["o3n_mm"], 1)

            def a3(t):
                pe.wait_ge(S["proT2"], t + 1)
                product3(bank[4], proT[2], h3, NT, NT).then_inc(S["av3_mm"], 1)

            def x3_(t):
                pe.wait_ge(S["xn2"], t + 1)
                transposes(bank[4], xn[2]).then_inc(S["xnT2_mm"], 1)

            def q4(t):
                pe.wait_ge(S["xnT2"], t + 1)
                wait(pe, S["o4T"], t)
                product3(bank[6], WP["wqT"], xnT[2], CT, CT).then_inc(S["q4_mm"], 1)

            def k4(t):
                wait(pe, S["y3"], t)
                product3(bank[7], WP["wkT"], xnT[2], CT, CT).then_inc(S["k4_mm"], 1)

            def v4_(t):
                pe.wait_ge(S["qT"], t + 1)
                product3(bank[6], xnT[2], WP["wvT"], CT, NT).then_inc(S["v4_mm"], 1)

            def scores(h):
                for g in (h, h + 1):
                    nc.tensor.matmul(bank[7 - g % 2][:, :, :], ident16[:, :], mask3[:, :, :], start=True, stop=False)
                for m in range(NT):
                    for g in (h, h + 1):
                        rows_ = slice((g % 2) * HD, (g % 2) * HD + HD)
                        for i, (a, b) in enumerate(((0, 1), (1, 0), (0, 0))):
                            ins = nc.tensor.matmul(bank[7 - g % 2][:, m, :], qT[a][rows_, g // 2, m * P:(m + 1) * P], kT[b][rows_, g // 2, :],
                                                   start=False, stop=(m == NT - 1 and i == 2))
                ins.then_inc(S["sc4_mm"], 1)

            def s40(t):
                pe.wait_ge(S["kT"], t + 1)
                pe.wait_ge(S["v4"], t + 1)
                scores(0)

            def s42(t):
                pe.wait_ge(S["p4T"], HEADS * t + 2)
                scores(2)

            def t4(h):
                def step(t):
                    pe.wait_ge(S["p4n"], HEADS * t + h + 1)
                    transposes(bank[7 - h % 2], p4[:, h % 2, :, :]).then_inc(S["p4T_mm"], 1)
                return step

            def a4(t):
                pe.wait_ge(S["p4T"], HEADS * t + HEADS)
                for c in range(CT):
                    for k in range(NT):
                        for g in range(2):
                            h = 2 * c + g
                            ins = nc.tensor.matmul(bank[6][g * HD:(g + 1) * HD, c, :], v4[:, k, h * HD:(h + 1) * HD], p4T[:, h, k, :],
                                                   start=(k == 0), stop=(k == NT - 1))
                ins.then_inc(S["av4_mm"], 1)

            def y4(t):
                pe.wait_ge(S["o4T"], t + 1)
                product3(bank[7], o4T, WP["woT"], CT, NT).then_inc(S["y4_mm"], 1)

            run(pe, ORDERS["pe"], {"g0": g0, "h0": h0_, "s0": s0, "t0": t0, "a0": a0, "x0": x0_,
                     "h1": h1_, "f1": f1_, "u1": u1_, "t1": t1, "a1": a1, "x1": x1_,
                     "m2": m2, "f2": f2, "b2": b2, "c2": c2, "r2": r2, "d2": d2, "v2": v2, "vb2": vb2, "on3": on3,
                     "m3": m3, "h3": h3_, "f3": f3_, "u3": u3_, "t3": t3, "a3": a3, "x3": x3_,
                     "q4": q4, "k4": k4, "v4": v4_, "s40": s40, "s42": s42,
                     "t40": t4(0), "t41": t4(1), "t42": t4(2), "t43": t4(3), "a4": a4, "y4": y4})

        @block.scalar
        def _(ac):
            def copy(dst, src):
                return nc.scalar.activation(dst, src, ACT.Copy)

            def exps(i):
                for m in range(NT):
                    ins = nc.scalar.activation(pro[i][:, m, :], sco[i][:, m, :], ACT.Exp, bias=nmax[i][:, m:m + 1], accum_out=den[i][:, m:m + 1])
                return ins

            def select(dst, src, c):
                return nc.scalar.activation(dst, src, ACT.Identity, scale=ident[0:2, c:c + 1], bias=ident[0:2, 1 - c:2 - c])

            ac.wait_ge(S["made"], 1)

            def g0(t):
                ac.wait_ge(S["g0_mm"], t + 1)
                copy(gT[0][:, :, :], bank[0][:, :, :]).then_inc(S["g0h"], 1)

            def h0_(t):
                ac.wait_ge(S["h0_mm"], t + 1)
                copy(h0[0][:, :, :], bank[0][:, :, :]).then_inc(S["h0h"], 1)

            def h1_(t):
                ac.wait_ge(S["h1_mm"], t + 1)
                copy(h1[0][:, :, :], bank[1][:, :, :]).then_inc(S["h1h"], 1)

            def h3_(t):
                ac.wait_ge(S["h3_mm"], t + 1)
                copy(h3[0][:, :, :], bank[5][:, :, :]).then_inc(S["h3h"], 1)

            def w2(t):
                ac.wait_ge(S["pfcTf"], t + 1)
                ac.wait_ge(S["hfc_mm"], 2 * t + 2)
                copy(pfcTp[0], pfcT[:, :, :]).then_inc(S["pfcTh"], 1)

            def j2(t):
                wait(ac, S["y2"], t)
                ac.wait_ge(S["xn1"], t + 1)
                copy(x2b[:, :, :], xn[1][:, :, :]).then_inc(S["x2b"], 1)

            def l2(t):
                ac.wait_ge(S["x0T_in"], 16 * (t + 1))
                wait(ac, S["s0_mm"], t)
                copy(x0Tp[0][:, :, :], x0T[:, :, :]).then_inc(S["x0Th"], 1)

            def s0(t):
                ac.wait_ge(S["s0_mm"], t + 1)
                copy(raw[0][:, :, :], bank[0][:, :, :]).then_inc(S["raw0"], 1)

            def p0(t):
                ac.wait_ge(S["nmax0"], 2 * t + 2)
                exps(0).then_inc(S["pro0"], 1)

            def t0(t):
                ac.wait_ge(S["proT0_mm"], t + 1)
                copy(proT[0][0][:, :, :], bank[0][:, :, :]).then_inc(S["proT0h"], 1)

            def a0(t):
                ac.wait_ge(S["av0_mm"], t + 1)
                ac.wait_ge(S["rden0"], t + 1)
                for m in range(NT):
                    ins = nc.scalar.activation(act[0][:, m, :], bank[0][:, m, :], ACT.Relu, scale=rden[0][:, m:m + 1])
                ins.then_inc(S["act0"], 1)

            def x0_(t):
                ac.wait_ge(S["xnT0_mm"], t + 1)
                copy(xnT[0][0][:, :, :], bank[0][:, :, :]).then_inc(S["xnT0h"], 1)

            def f1_(t):
                ac.wait_ge(S["f1_mm"], t + 1)
                select(src1, bank[1][0:2, 0, :], 0)
                select(dst1, bank[1][0:2, 0, :], 1).then_inc(S["rows1"], 1)

            def u1_(t):
                ac.wait_ge(S["u1_mm"], t + 1)
                copy(raw[1][:, :, :], bank[1][:, :, :]).then_inc(S["raw1"], 1)

            def p1(t):
                ac.wait_ge(S["nmax1"], 2 * t + 2)
                exps(1).then_inc(S["pro1"], 1)

            def t1(t):
                ac.wait_ge(S["proT1_mm"], t + 1)
                copy(proT[1][0][:, :, :], bank[1][:, :, :]).then_inc(S["proT1h"], 1)

            def a1(t):
                ac.wait_ge(S["av1_mm"], t + 1)
                ac.wait_ge(S["rden1"], t + 1)
                for m in range(NT):
                    ins = nc.scalar.activation(act[1][:, m, :], bank[1][:, m, :], ACT.Exp, scale=rden[1][:, m:m + 1])
                ins.then_inc(S["act1"], 1)

            def x1_(t):
                ac.wait_ge(S["xnT1_mm"], t + 1)
                copy(xnT[1][0][:, :, :], bank[1][:, :, :]).then_inc(S["xnT1h"], 1)

            def m2(t):
                ac.wait_ge(S["o1_mm"], t + 1)
                for m in range(HT):
                    ins = nc.scalar.activation(o1T[:, m, :], bank[2 + m // 2][:, m % 2, :], ACT.Relu, bias=W["b1"][:, m, 0:1])
                ins.then_inc(S["o1T"], 1)
                ac.wait_ge(S["o1T"], t + 1)
                copy(o1Tp[0][:, :, :], o1T[:, :, :]).then_inc(S["o1Th"], 1)

            def f2(t):
                ac.wait_ge(S["ffc_mm"], t + 1)
                copy(ffc, bank[2][0:2, 0, :]).then_inc(S["ffcr"], 1)

            def c2(t):
                ac.wait_ge(S["hfc_mm"], 2 * t + 1)
                copy(hfc[0][:, 0, :].rearrange("p (a b) -> p a b", a=2), bank[3][:, :, :]).then_inc(S["hfch"], 1)

            def rc2(t):
                ac.wait_ge(S["np"], t + 1)
                nc.scalar.activation(rows[:, 0, :], neg_pos[:, 0, :], ACT.Exp, scale=1.0 - SLOPE)
                nc.scalar.activation(rows[:, 1, :], neg_pos[:, 1, :], ACT.Exp, scale=-(1.0 - SLOPE)).then_inc(S["rows"], 1)
                ac.wait_ge(S["gap"], t + 1)
                nc.scalar.activation(cols[:, 0, :], gap[:, :], ACT.Exp)
                nc.scalar.activation(cols[:, 1, :], gap[:, :], ACT.Exp, scale=SLOPE).then_inc(S["cols"], 1)

            def r2(t):
                ac.wait_ge(S["hfc_mm"], 2 * t + 2)
                copy(hfc[0][:, 1, :].rearrange("p (a b) -> p a b", a=2), bank[3][:, :, :]).then_inc(S["hfch"], 1)

            def y2(t):
                ac.wait_ge(S["cut"], t + 1)
                nc.scalar.activation(ex1[:, :, :], cut[:, :, :], ACT.Exp).then_inc(S["ex1"], 1)
                ac.wait_ge(S["ex1"], t + 1)
                nc.scalar.activation(ex2[:, :, :], ex1[:, :, :], ACT.Exp, bias=W["m1"][:, 0, 0:1]).then_inc(S["ex2"], 1)

            def z2(t):
                ac.wait_ge(S["o2"], t + 1)
                wait(ac, S["o3_mm"], t)
                copy(o2T[0][:, :, :], o2[:, :, :]).then_inc(S["o2Th"], 1)

            def m3(t):
                ac.wait_ge(S["o3_mm"], t + 1)
                for m in range(CT):
                    ins = nc.scalar.activation(o3T[:, m, :], bank[4][:, m, :], ACT.Relu, bias=b2m[:, m:m + 1])
                ins.then_inc(S["o3T"], 1)
                ac.wait_ge(S["o3T"], t + 1)
                copy(o3Tp[0][:, :, :], o3T[:, :, :]).then_inc(S["o3Th"], 1)

            def f3_(t):
                ac.wait_ge(S["f3_mm"], t + 1)
                select(src3, bank[4][0:2, 0, :], 0)
                select(dst3, bank[4][0:2, 0, :], 1).then_inc(S["rows3"], 1)

            def u3_(t):
                ac.wait_ge(S["u3_mm"], t + 1)
                copy(raw[2][:, :, :], bank[4][:, :, :]).then_inc(S["raw2"], 1)

            def p3(t):
                ac.wait_ge(S["nmax2"], 2 * t + 2)
                exps(2).then_inc(S["pro2"], 1)

            def t3(t):
                ac.wait_ge(S["proT2_mm"], t + 1)
                copy(proT[2][0][:, :, :], bank[4][:, :, :]).then_inc(S["proT2h"], 1)

            def a3(t):
                ac.wait_ge(S["cut3"], t + 1)
                nc.scalar.activation(act[2][:, :, :], cut3[:, :, :], ACT.Exp).then_inc(S["act2"], 1)
                ac.wait_ge(S["act2"], t + 1)
                nc.scalar.activation(act[2][:, :, :], act[2][:, :, :], ACT.Exp, bias=W["m1"][:, 0, 0:1]).then_inc(S["ex3"], 1)

            def x3_(t):
                ac.wait_ge(S["xnT2_mm"], t + 1)
                copy(xnT[2][0][:, :, :], bank[4][:, :, :]).then_inc(S["xnT2h"], 1)

            def q4(t):
                ac.wait_ge(S["q4_mm"], t + 1)
                for m in range(CT):
                    ins = nc.scalar.activation(qT[0][:, m, :], bank[6][:, m, :], ACT.Identity, bias=bq8[:, m:m + 1])
                ins.then_inc(S["qTh"], 1)

            def k4(t):
                ac.wait_ge(S["k4_mm"], t + 1)
                for m in range(CT):
                    ins = nc.scalar.activation(kT[0][:, m, :], bank[7][:, m, :], ACT.Identity, bias=W["bk"][:, m, 0:1])
                ins.then_inc(S["kTh"], 1)

            def p4_(h):
                def step(t):
                    ac.wait_ge(S["nmx4"], HEADS * t + h + 1)
                    for m in range(NT):
                        ins = nc.scalar.activation(p4[:, h % 2, m, :], bank[7 - h % 2][:, m, :], ACT.Exp,
                                                   bias=nmx4[:, h, m:m + 1], accum_out=den4[:, h, m:m + 1])
                    ins.then_inc(S["p4"], 1)
                return step

            def t4(h):
                def step(t):
                    ac.wait_ge(S["p4T_mm"], HEADS * t + h + 1)
                    copy(p4T[:, h, :, :], bank[7 - h % 2][:, :, :]).then_inc(S["p4T"], 1)
                return step

            def a4(t):
                ac.wait_ge(S["av4_mm"], t + 1)
                copy(o4T[0][:, :, :], bank[6][:, :, :]).then_inc(S["o4Th"], 1)

            run(ac, ORDERS["ac"], {"h0": h0_, "h1": h1_, "h3": h3_, "w2": w2, "j2": j2, "l2": l2, "g0": g0, "s0": s0, "p0": p0, "t0": t0, "a0": a0, "x0": x0_,
                     "f1": f1_, "f3": f3_, "u1": u1_, "p1": p1, "t1": t1, "a1": a1, "x1": x1_,
                     "m2": m2, "f2": f2, "c2": c2, "rc2": rc2, "r2": r2, "y2": y2, "z2": z2,
                     "m3": m3, "u3": u3_, "p3": p3, "t3": t3, "a3": a3, "x3": x3_,
                     "q4": q4, "k4": k4, "p40": p4_(0), "p41": p4_(1), "p42": p4_(2), "p43": p4_(3),
                     "t40": t4(0), "t41": t4(1), "t42": t4(2), "t43": t4(3), "a4": a4})

        @block.vector
        def _(dv):
            V = nc.vector

            def low_part(pair, whole):
                return V.tensor_tensor(pair[1][:, :, :], whole, pair[0][:, :, :].bitcast(fp32), ALU.subtract)

            dv.wait_ge(S["loaded"], 16 * n_loads)
            V.tensor_copy(ident16[:, :], ident[:, :])
            V.tensor_scalar(mask16[:, :, :], adj_sb, 0.0, MASK, ALU.is_le, ALU.mult)
            V.tensor_scalar(mask3[:, :, :], adj_sb, 0.0, MASK, ALU.is_equal, ALU.mult).then_inc(S["setup_dve"], 1)
            dv.wait_ge(S["setup_dve"], 1)
            V.reduce_max(some3[:, :], mask3[:, :, :], AX.X).then_inc(S["setup_dve"], 1)
            dv.wait_ge(S["setup_dve"], 2)
            V.tensor_scalar(some3[:, :], some3[:, :], 0.0, None, ALU.is_equal)
            V.tensor_scalar(bq8[:, :], W["bq"][:, :, 0], QSCALE, None, ALU.mult)
            V.tensor_scalar(W["wqT"], W["wqT"], QSCALE, None, ALU.mult).then_inc(S["setup_dve"], 1)
            dv.wait_ge(S["setup_dve"], 3)
            for n in SPLIT:
                ins = V.tensor_copy(WP[n][0][:, :, :], W[n])
            ins.then_inc(S["wsplit"], 1)
            dv.wait_ge(S["wsplit"], 1)
            for n in SPLIT:
                low_part(WP[n], W[n])
            dv.wait_ge(S["setup_pool"], 1)
            V.tensor_copy(ones2[:, :], ones[:, :])
            dv.wait_ge(S["setup_pe"], 1)
            V.tensor_copy(A0f[:, :, :], bank[0][:, :, :]).then_inc(S["setup_dve"], 1)
            dv.wait_ge(S["setup_dve"], 4)
            results = ((A0, A0f[:, :, :]), (v1, bank[1][:, :, 0:2]), (vha, bank[2][:, :, 0:2]),
                       (vfc, bank[3][:, 0, 0:2 * HT].rearrange("p (m c) -> p m c", c=2)))
            for pair, whole in results:
                ins = V.tensor_copy(pair[0][:, :, :], whole)
            ins.then_inc(S["wsplit"], 1)
            dv.wait_ge(S["wsplit"], 2)
            for pair, whole in results:
                low_part(pair, whole)
            V.tensor_tensor(b2m[:, :], W["b2"][:, :, 0], bank[4][:, 0, 0:CT], ALU.subtract).then_inc(S["made"], 1)

            def leaky(i, s, a, b, t):
                V.scalar_tensor_tensor(sco[i][:, :, :], a, SLOPE, b, ALU.mult, ALU.max).then_inc(s, 1)
                dv.wait_ge(s, 2 * t + 1)
                V.tensor_reduce(nmax[i][:, :], sco[i][:, :, :], AX.X, ALU.max, negate=True).then_inc(s, 1)

            def stats(i, s_y, s_mv, t):
                dv.wait_ge(s_y, t + 1)
                for m in range(NT):
                    ins = V.bn_stats(stat[i][:, m, :], y[i][:, m, :])
                ins.then_inc(s_mv, 1)
                dv.wait_ge(S["loaded"], 16)
                dv.wait_ge(s_mv, 2 * t + 1)
                for m in range(NT):
                    ins = V.bn_aggr(mv[i][:, m, :], stat[i][:, m, :])
                ins.then_inc(s_mv, 1)

            def norm(i):
                for m in range(NT):
                    ins = V.tensor_scalar(xn[i][:, m, :], y[i][:, m, :], mv[i][:, m, 0:1], rstd[i][:, m:m + 1], ALU.subtract, ALU.mult)
                return ins

            def g0(t):
                dv.wait_ge(S["g0h"], t + 1)
                low_part(gT, bank[0][:, :, :]).then_inc(S["g0"], 1)

            def x0_(t):
                dv.wait_ge(S["xnT0h"], t + 1)
                low_part(xnT[0], bank[0][:, :, :]).then_inc(S["xnT0"], 1)

            def hidden_low(m):
                def step(t):
                    dv.wait_ge(S["hfch"], 2 * t + m + 1)
                    V.tensor_tensor(hfc[1][:, m, :], bank[3][:, :, :].rearrange("p a b -> p (a b)"), hfc[0][:, m, :].bitcast(fp32),
                                    ALU.subtract).then_inc(S["hfc"], 1)
                return step

            def p4_(h):
                def step(t):
                    dv.wait_ge(S["p4"], HEADS * t + h + 1)
                    V.reciprocal(den4[:, h, :], den4[:, h, :]).then_inc(S["rd4a"], 1)
                return step

            def a4(t):
                dv.wait_ge(S["o4Th"], t + 1)
                low_part(o4T, bank[6][:, :, :]).then_inc(S["o4T"], 1)

            def x1_(t):
                dv.wait_ge(S["xnT1h"], t + 1)
                low_part(xnT[1], bank[1][:, :, :]).then_inc(S["xnT1"], 1)

            def x3_(t):
                dv.wait_ge(S["xnT2h"], t + 1)
                low_part(xnT[2], bank[4][:, :, :]).then_inc(S["xnT2"], 1)

            def z2(t):
                dv.wait_ge(S["o2Th"], t + 1)
                low_part(o2T, o2[:, :, :]).then_inc(S["o2T"], 1)

            def h0_(t):
                dv.wait_ge(S["h0h"], t + 1)
                low_part(h0, bank[0][:, :, :]).then_inc(S["h0"], 1)

            def s0(t):
                dv.wait_ge(S["raw0"], t + 1)
                leaky(0, S["nmax0"], bank[0][:, :, :], raw[0][:, :, :], t)

            def t0(t):
                dv.wait_ge(S["pro0"], t + 1)
                V.reciprocal(rden[0][:, :], den[0][:, :]).then_inc(S["rden0"], 1)
                dv.wait_ge(S["proT0h"], t + 1)
                low_part(proT[0], bank[0][:, :, :]).then_inc(S["proT0"], 1)

            def st0(t):
                stats(0, S["y0"], S["mv0"], t)

            def n0(t):
                dv.wait_ge(S["rstd0"], 2 * t + 2)
                wait(dv, S["y1"], t)
                norm(0).then_inc(S["xn0"], 1)

            def h1_(t):
                dv.wait_ge(S["h1h"], t + 1)
                low_part(h1, bank[1][:, :, :]).then_inc(S["h1"], 1)

            def e1_(t):
                dv.wait_ge(S["raw1"], t + 1)
                leaky(1, S["nmax1"], bank[1][:, :, :], raw[1][:, :, :], t)

            def t1(t):
                dv.wait_ge(S["pro1"], t + 1)
                V.reciprocal(rden[1][:, :], den[1][:, :]).then_inc(S["rden1"], 1)
                dv.wait_ge(S["proT1h"], t + 1)
                low_part(proT[1], bank[1][:, :, :]).then_inc(S["proT1"], 1)

            def a1(t):
                dv.wait_ge(S["act1"], t + 1)
                for m in range(NT):
                    ins = V.tensor_scalar(q1[:, m, :], bank[1][:, m, :], rden[1][:, m:m + 1], 0.0, ALU.mult, ALU.max)
                ins.then_inc(S["e1"], 1)
                dv.wait_ge(S["e1"], 2 * t + 1)
                V.scalar_tensor_tensor(e1[:, :, :], act[1][:, :, :], 1.0, q1[:, :, :], ALU.min, ALU.add).then_inc(S["e1"], 1)

            def st1(t):
                stats(1, S["y1"], S["mv1"], t)

            def n1(t):
                dv.wait_ge(S["rstd1"], 2 * t + 2)
                wait(dv, S["x2b"], t)
                norm(1).then_inc(S["xn1"], 1)

            def f2(t):
                dv.wait_ge(S["ffcr"], t + 1)
                V.reduce_max(fmax_row[:, :], ffc, AX.X).then_inc(S["fmaxr"], 1)

            def b2(t):
                dv.wait_ge(S["b2_mm"], t + 1)
                V.tensor_copy(fmax[:, :], bank[2][:, 1, 0:1]).then_inc(S["fmax"], 1)
                dv.wait_ge(S["fmax"], t + 1)
                V.tensor_scalar(neg_pos[:, 0, :], bank[2][:, 0, :], fmax[:, 0:1], 0.0, ALU.add, ALU.min)
                V.tensor_scalar(neg_pos[:, 1, :], bank[2][:, 0, :], fmax[:, 0:1], 0.0, ALU.add, ALU.max).then_inc(S["np"], 1)
                V.tensor_scalar(gap[:, :], bank[2][:, 1, 2:2 + 2 * NT].rearrange("p (m c) -> p m c", c=2)[:, :, 1], fmax[:, 0:1], None, ALU.subtract).then_inc(S["gap"], 1)

            def w2(t):
                dv.wait_ge(S["rows"], t + 1)
                dv.wait_ge(S["cols"], t + 1)
                for m in range(NT):
                    ins = V.tensor_scalar(low[:, m, :], rows[:, 1, :], cols[:, 1, m:m + 1], None, ALU.mult)
                ins.then_inc(S["low"], 1)
                dv.wait_ge(S["low"], t + 1)
                for m in range(NT):
                    ins = V.scalar_tensor_tensor(pfcT[:, m, :], rows[:, 0, :], cols[:, 0, m:m + 1], low[:, m, :], ALU.mult, ALU.max)
                ins.then_inc(S["pfcTf"], 1)

            def v2(t):
                dv.wait_ge(S["den2_mm"], t + 1)
                V.reciprocal(rdb[:, :], bank[2][:, 0, :]).then_inc(S["rdb"], 1)
                dv.wait_ge(S["rdb"], t + 1)
                rb = rdb[:, :].unsqueeze(1).broadcast_to([P, 2, N])
                dv.wait_ge(S["av2a_mm"], t + 1)
                V.tensor_tensor(att[:, 0:2, :], bank[3][:, :, :], rb, ALU.mult)

            def vb2(t):
                rb = rdb[:, :].unsqueeze(1).broadcast_to([P, 2, N])
                dv.wait_ge(S["av2b_mm"], t + 1)
                V.tensor_tensor(att[:, 2:4, :], bank[2][:, :, :], rb, ALU.mult).then_inc(S["att_b"], 1)

            def i2(t):
                dv.wait_ge(S["att_b"], t + 1)
                V.tensor_scalar(cut[:, :, :], att[:, :, :], 0.0, None, ALU.min).then_inc(S["cut"], 1)
                V.scalar_tensor_tensor(res[:, :, :], att[:, :, :], 0.0, o1T[:, :, :], ALU.max, ALU.add).then_inc(S["res"], 1)

            def h3_(t):
                dv.wait_ge(S["h3h"], t + 1)
                low_part(h3, bank[5][:, :, :]).then_inc(S["h3"], 1)

            def e3_(t):
                dv.wait_ge(S["raw2"], t + 1)
                leaky(2, S["nmax2"], bank[4][:, :, :], raw[2][:, :, :], t)

            def t3(t):
                dv.wait_ge(S["pro2"], t + 1)
                V.reciprocal(rden[2][:, :], den[2][:, :]).then_inc(S["rden2"], 1)
                dv.wait_ge(S["proT2h"], t + 1)
                low_part(proT[2], bank[4][:, :, :]).then_inc(S["proT2"], 1)

            def a3(t):
                dv.wait_ge(S["rden2"], t + 1)
                dv.wait_ge(S["av3_mm"], t + 1)
                for m in range(NT):
                    ins = V.tensor_scalar(cut3[:, m, :], bank[4][:, m, :], rden[2][:, m:m + 1], 0.0, ALU.mult, ALU.min)
                ins.then_inc(S["cut3"], 1)
                for m in range(NT):
                    ins = V.tensor_scalar(q3[:, m, :], bank[4][:, m, :], rden[2][:, m:m + 1], 0.0, ALU.mult, ALU.max)
                ins.then_inc(S["q3"], 1)

            def r3_(t):
                dv.wait_ge(S["q3"], t + 1)
                dv.wait_ge(S["o3n_mm"], t + 1)
                V.scalar_tensor_tensor(r3[:, :, :], q3[:, :, :], -1.0, bank[5][:, :, :], ALU.add, ALU.add).then_inc(S["r3"], 1)

            def z3(t):
                dv.wait_ge(S["e3"], t + 1)
                dv.wait_ge(S["x2b"], t + 1)
                V.scalar_tensor_tensor(y[2][:, :, :], e3[:, :, :], 0.0, x2b[:, :, :], ALU.max, ALU.add).then_inc(S["y2"], 1)

            def st3(t):
                stats(2, S["y2"], S["mv2"], t)

            def n3(t):
                dv.wait_ge(S["rstd2"], 2 * t + 2)
                wait(dv, S["xb4"], t)
                norm(2).then_inc(S["xn2"], 1)

            def q4(t):
                dv.wait_ge(S["qTh"], t + 1)
                for m in range(CT):
                    ins = V.scalar_tensor_tensor(qT[1][:, m, :], bank[6][:, m, :], bq8[:, m:m + 1], qT[0][:, m, :].bitcast(fp32), ALU.add, ALU.subtract)
                ins.then_inc(S["qT"], 1)

            def k4(t):
                dv.wait_ge(S["kTh"], t + 1)
                for m in range(CT):
                    ins = V.scalar_tensor_tensor(kT[1][:, m, :], bank[7][:, m, :], W["bk"][:, m, 0:1], kT[0][:, m, :].bitcast(fp32), ALU.add, ALU.subtract)
                ins.then_inc(S["kT"], 1)

            def v4_(t):
                dv.wait_ge(S["v4_mm"], t + 1)
                V.tensor_tensor(v4[:, :, :], bank[6][:, :, :], W["bv"][:, 0:1, :].broadcast_to([P, NT, C]), ALU.add).then_inc(S["v4"], 1)

            def s4(h):
                def step(t):
                    dv.wait_ge(S["sc4_mm"], HEADS // 2 * t + h // 2 + 1)
                    V.tensor_reduce(nmx4[:, h, :], bank[7 - h % 2][:, :, :], AX.X, ALU.max, negate=True).then_inc(S["nmx4"], 1)
                return step

            def y4(t):
                dv.wait_ge(S["y4_mm"], t + 1)
                dv.wait_ge(S["xb4"], t + 1)
                V.tensor_tensor(y[3][:, :, :], bank[7][:, :, :], xb4[:, :, :], ALU.add).then_inc(S["y3"], 1)

            def st4(t):
                stats(3, S["y3"], S["mv3"], t)

            def n4(t):
                dv.wait_ge(S["rstd3"], 2 * t + 2)
                wait(dv, S["stored"], 16 * t)
                norm(3).then_inc(S["xn3"], 1)

            run(dv, ORDERS["dv"], {"g0": g0, "x0": x0_, "c2": hidden_low(0), "r2": hidden_low(1), "x1": x1_, "x3": x3_, "z2": z2, "h0": h0_, "s0": s0, "t0": t0, "st0": st0, "n0": n0,
                     "h1": h1_, "e1": e1_, "t1": t1, "a1": a1, "st1": st1, "n1": n1,
                     "f2": f2, "b2": b2, "w2": w2, "v2": v2, "vb2": vb2, "i2": i2,
                     "h3": h3_, "e3": e3_, "t3": t3, "a3": a3, "r3": r3_, "z3": z3, "st3": st3, "n3": n3,
                     "q4": q4, "k4": k4, "v4": v4_, "s40": s4(0), "s41": s4(1), "s42": s4(2), "s43": s4(3), "p40": p4_(0), "p41": p4_(1), "p42": p4_(2), "p43": p4_(3), "a4": a4, "y4": y4, "st4": st4, "n4": n4})

        @block.gpsimd
        def _(po):
            G = nc.gpsimd
            G.memset(eps[:, :], EPS)
            G.memset(mhalf[:, :], -0.5)
            G.memset(ones[:, :], 1.0).then_inc(S["setup_pool"], 1)
            po.wait_ge(S["setup_pool"], 1)
            po.wait_ge(S["made"], 1)

            def inv_std(i, s_mv, s_rs, t):
                po.wait_ge(s_mv, 2 * t + 2)
                G.tensor_tensor(vare[i][:, :], mv[i][:, :, 1], eps[:, :], ALU.add).then_inc(s_rs, 1)
                po.wait_ge(s_rs, 2 * t + 1)
                G.tensor_tensor(rstd[i][:, :], vare[i][:, :], mhalf[:, :], ALU.pow).then_inc(s_rs, 1)

            def a0(t):
                po.wait_ge(S["x0_in"], 16 * (t + 1))
                po.wait_ge(S["act0"], t + 1)
                G.tensor_tensor(y[0][:, :, :], act[0][:, :, :], x0[:, :, :], ALU.add).then_inc(S["y0"], 1)

            def st0(t):
                inv_std(0, S["mv0"], S["rstd0"], t)

            def y1(t):
                po.wait_ge(S["e1"], 2 * t + 2)
                G.tensor_tensor(y[1][:, :, :], e1[:, :, :], xn[0][:, :, :], ALU.add).then_inc(S["y1"], 1)

            def st1(t):
                inv_std(1, S["mv1"], S["rstd1"], t)

            def z2(t):
                po.wait_ge(S["ex2"], t + 1)
                po.wait_ge(S["res"], t + 1)
                wait(po, S["o2T"], t)
                G.tensor_tensor(o2[:, :, :], ex2[:, :, :], res[:, :, :], ALU.add).then_inc(S["o2"], 1)

            def m2(t):
                po.wait_ge(S["o1Th"], t + 1)
                G.tensor_tensor(o1Tp[1][:, :, :], o1T[:, :, :], o1Tp[0][:, :, :].bitcast(fp32), ALU.subtract).then_inc(S["o1Tl"], 1)

            def l2(t):
                po.wait_ge(S["x0Th"], t + 1)
                G.tensor_tensor(x0Tp[1][:, :, :], x0T[:, :, :], x0Tp[0][:, :, :].bitcast(fp32), ALU.subtract).then_inc(S["x0Tl"], 1)

            def a3(t):
                po.wait_ge(S["ex3"], t + 1)
                po.wait_ge(S["r3"], t + 1)
                G.tensor_tensor(e3[:, :, :], act[2][:, :, :], r3[:, :, :], ALU.add).then_inc(S["e3"], 1)

            def st3(t):
                inv_std(2, S["mv2"], S["rstd2"], t)

            def w2(t):
                po.wait_ge(S["pfcTh"], t + 1)
                G.tensor_tensor(pfcTp[1], pfcT[:, :, :], pfcTp[0].bitcast(fp32), ALU.subtract).then_inc(S["pfcT"], 1)

            def m3(t):
                po.wait_ge(S["o3Th"], t + 1)
                G.tensor_tensor(o3Tp[1][:, :, :], o3T[:, :, :], o3Tp[0][:, :, :].bitcast(fp32), ALU.subtract).then_inc(S["o3Tl"], 1)

            def k4(t):
                wait(po, S["stored"], 16 * t)
                po.wait_ge(S["xn2"], t + 1)
                G.tensor_tensor(xb4[:, :, :], xn[2][:, :, :], W["bo"][:, 0:1, :].broadcast_to([P, NT, C]), ALU.add).then_inc(S["xb4"], 1)

            def p4_(h):
                def step(t):
                    po.wait_ge(S["rd4a"], HEADS * t + h + 1)
                    G.tensor_tensor(rd4[:, h, :], some3[:, :], den4[:, h, :], ALU.mult).then_inc(S["rd4"], 1)
                    po.wait_ge(S["rd4"], HEADS * t + h + 1)
                    G.tensor_tensor(p4[:, h % 2, :, :], p4[:, h % 2, :, :], rd4[:, h, :].unsqueeze(2).broadcast_to([P, NT, N]),
                                    ALU.mult).then_inc(S["p4n"], 1)
                return step

            def st4(t):
                inv_std(3, S["mv3"], S["rstd3"], t)

            run(po, ORDERS["po"], {"m2": m2, "l2": l2, "a0": a0, "st0": st0, "y1": y1, "st1": st1, "z2": z2, "a3": a3, "st3": st3, "t41": k4, "p40": p4_(0), "p41": p4_(1), "p42": p4_(2), "p43": p4_(3), "st4": st4, "w2": w2, "m3": m3})


def kernel(**inputs):
    import numpy as np
    import concourse.bacc as bacc
    from concourse.bass_utils import run_bass_kernel_spmd

    a = {n: np.asarray(v) for n, v in inputs.items()}
    x = a["x"]
    column = lambda v: v.reshape(-1, 1)
    spread = lambda v: np.repeat(v.reshape(1, -1), P, axis=0)
    layout = {
        "W1T": a["L0_gnn_W1"].T, "W2T": a["L0_gnn_W2"].T, "W3": a["L0_gnn_W3"],
        "W_": a["L1_gnn_W"], "W_T": a["L1_gnn_W"].T, "a1": a["L1_gnn_a"].reshape(2, -1).T,
        "mlp1": a["L2_gnn_mlp1_w"], "b1": column(a["L2_gnn_mlp1_b"]),
        "fc": a["L2_gnn_W_fc"], "fc_T": a["L2_gnn_W_fc"].T, "afc": a["L2_gnn_a_fc"].reshape(2, -1).T,
        "mlp2": a["L2_gnn_mlp2_w"], "b2": column(a["L2_gnn_mlp2_b"]),
        "hand": a["L2_gnn_W_hand"], "hand_T": a["L2_gnn_W_hand"].T, "ahand": a["L2_gnn_a_hand"].reshape(2, -1).T,
        "wqT": a["L3_gnn_wq"].T, "bq": column(a["L3_gnn_bq"]),
        "wkT": a["L3_gnn_wk"].T, "bk": column(a["L3_gnn_bk"]),
        "wvT": a["L3_gnn_wv"].T, "bv": spread(a["L3_gnn_bv"]),
        "woT": a["L3_gnn_wo"].T, "bo": spread(a["L3_gnn_bo"]),
        "m1": np.full((P, 1), -1.0, np.float32),
    }
    nc = bacc.Bacc("TRN2", target_bir_lowering=False, num_devices=1)
    arrays = {}

    def dram(name, v):
        arrays[name] = np.ascontiguousarray(v)
        return nc.dram_tensor(name, v.shape, mybir.dt.from_np(v.dtype), kind="ExternalInput").ap()

    tiled = lambda v: np.swapaxes(v.reshape(*v.shape[:-2], -1, P, v.shape[-1]), -3, -2)
    weights = {n: dram("in_" + n, tiled(v)) for n, v in layout.items()}
    ins = [dram("in_x", tiled(x)), dram("in_xT", tiled(np.transpose(x, (0, 2, 1)))), dram("in_adj", tiled(a["adj"])),
           dram("in_ident", np.eye(P, dtype=np.float32))]
    out = nc.dram_tensor("out", x.shape, mybir.dt.from_np(x.dtype), kind="ExternalOutput").ap()
    graph_stack(nc, *ins, weights, out)
    return run_bass_kernel_spmd(nc, [arrays], core_ids=[0]).results[0]["out"]
```
